# Optimizing a Trainium2 kernel written in Bass

```python
import numpy as np
import jax
import jax.numpy as jnp

def _softmax(x, axis=-1):
    return jax.nn.softmax(x, axis=axis)

def _gelu(x):
    return jax.nn.gelu(x, approximate=True)

def _silu(x):
    return jax.nn.silu(x)

def _sigmoid(x):
    return jax.nn.sigmoid(x)

def _layernorm(x, axis=-1, eps=1e-05):
    m = jnp.mean(x, axis=axis, keepdims=True)
    v = jnp.var(x, axis=axis, keepdims=True)
    return (x - m) / jnp.sqrt(v + eps)

def _scatter_add(tgt, idx, src, axis=0):
    return tgt.at[idx].add(src)

def _segment_sum(src, seg, n):
    return jax.ops.segment_sum(src, seg, n)
kernel_name = 'mk_prb_d1_jaxref_r8_792660'

def setup_inputs(seed: int=0):
    np.random.seed(seed)
    _w = jnp.asarray

    def _L0_attn_setup():
        import jax, jax.numpy as jnp
        import numpy as np
        B_, L_, D_ = (2, 128, 256)
        E_, N_, R_, K_ = (512, 16, 128, 4)
        EPS = 1e-05

        def _forward(resid, norm_w, skip_w, in_w, conv_w, conv_b, wd1, wd2, wd2_b, wB, wC, A_log, W_D, out_w):
            B, L, D = resid.shape
            E, K = conv_w.shape
            N = A_log.shape[1]
            rn = resid * jax.lax.rsqrt(jnp.mean(resid * resid, -1, keepdims=True) + EPS) * norm_w
            skip = rn @ skip_w.T
            x_in = rn @ in_w.T
            xp = jnp.pad(x_in, ((0, 0), (K - 1, 0), (0, 0)))
            conv = conv_b + sum((xp[:, k:k + L, :] * conv_w[:, k] for k in range(K)))
            x = jax.nn.silu(conv)
            delta = jax.nn.softplus(x @ wd1.T @ wd2.T + wd2_b)
            A = -jnp.exp(A_log)
            Bm = x @ wB.T
            Cm = x @ wC.T

            def step(h, inp):
                d_l, b_l, c_l, x_l = inp
                h = jnp.exp(d_l[:, :, None] * A) * h + (d_l * x_l)[:, :, None] * b_l[:, None, :]
                y_l = jnp.einsum('ben,bn->be', h, c_l)
                return (h, y_l)
            h0 = jnp.zeros((B, E, N), resid.dtype)
            xs = (delta.transpose(1, 0, 2), Bm.transpose(1, 0, 2), Cm.transpose(1, 0, 2), x.transpose(1, 0, 2))
            _, ys = jax.lax.scan(step, h0, xs)
            y = ys.transpose(1, 0, 2) + x * W_D
            y = y * jax.nn.silu(skip)
            return resid + y @ out_w.T
        key = jax.random.key(seed)
        ks = jax.random.split(key, 12)
        s = lambda i, shape, scale=0.02: jax.random.normal(ks[i], shape, jnp.float32) * scale
        dt = jnp.exp(jax.random.uniform(ks[10], (E_,)) * (np.log(0.1) - np.log(0.001)) + np.log(0.001))
        inv_dt = dt + jnp.log(-jnp.expm1(-dt))
        return {'resid': jax.random.normal(ks[0], (B_, L_, D_), jnp.float32), 'norm_w': jnp.ones((D_,), jnp.float32), 'skip_w': s(1, (E_, D_)), 'in_w': s(2, (E_, D_)), 'conv_w': s(3, (E_, K_), 0.2), 'conv_b': jnp.zeros((E_,), jnp.float32), 'wd1': s(4, (R_, E_)), 'wd2': s(5, (E_, R_), R_ ** (-0.5)), 'wd2_b': inv_dt, 'wB': s(6, (N_, E_)), 'wC': s(7, (N_, E_)), 'A_log': jnp.log(jnp.broadcast_to(jnp.arange(1, N_ + 1, dtype=jnp.float32), (E_, N_))), 'W_D': jnp.ones((E_,), jnp.float32), 'out_w': s(8, (D_, E_))}
    _L0_attn_in = _L0_attn_setup()

    def _L0_ffn_setup():
        import jax, jax.numpy as jnp
        import numpy as np
        D_MODEL = 256
        FFN_DIM = 512
        N_EXPERTS = 8
        TOP_K = 2
        key = jax.random.key(seed)
        ks = jax.random.split(key, 5)
        x = jax.random.normal(ks[0], (2, 128, D_MODEL), dtype=jnp.float32)
        Wr = jax.random.normal(ks[1], (D_MODEL, N_EXPERTS), dtype=jnp.float32) * 0.02
        W1 = jax.random.normal(ks[2], (N_EXPERTS, D_MODEL, FFN_DIM), dtype=jnp.float32) * 0.02
        V1 = jax.random.normal(ks[3], (N_EXPERTS, D_MODEL, FFN_DIM), dtype=jnp.float32) * 0.02
        W2 = jax.random.normal(ks[4], (N_EXPERTS, FFN_DIM, D_MODEL), dtype=jnp.float32) * 0.02
        return {'x': x, 'Wr': Wr, 'W1': W1, 'V1': V1, 'W2': W2}
    _L0_ffn_in = _L0_ffn_setup()
    _d = {'L0_attn_resid': _L0_attn_in['resid'], 'L0_attn_norm_w': _L0_attn_in['norm_w'], 'L0_attn_skip_w': _L0_attn_in['skip_w'], 'L0_attn_in_w': _L0_attn_in['in_w'], 'L0_attn_conv_w': _L0_attn_in['conv_w'], 'L0_attn_conv_b': _L0_attn_in['conv_b'], 'L0_attn_wd1': _L0_attn_in['wd1'], 'L0_attn_wd2': _L0_attn_in['wd2'], 'L0_attn_wd2_b': _L0_attn_in['wd2_b'], 'L0_attn_wB': _L0_attn_in['wB'], 'L0_attn_wC': _L0_attn_in['wC'], 'L0_attn_A_log': _L0_attn_in['A_log'], 'L0_attn_W_D': _L0_attn_in['W_D'], 'L0_attn_out_w': _L0_attn_in['out_w'], 'L0_ffn_Wr': _L0_ffn_in['Wr'], 'L0_ffn_W1': _L0_ffn_in['W1'], 'L0_ffn_V1': _L0_ffn_in['V1'], 'L0_ffn_W2': _L0_ffn_in['W2']}
    _x0 = _d['L0_attn_resid']
    _d['L0_attn_resid'] = jax.random.normal(jax.random.fold_in(jax.random.key(seed), 1), (4, 1024, 256), dtype=_x0.dtype)
    del _x0
    return _d

def reference(L0_attn_resid, L0_attn_norm_w, L0_attn_skip_w, L0_attn_in_w, L0_attn_conv_w, L0_attn_conv_b, L0_attn_wd1, L0_attn_wd2, L0_attn_wd2_b, L0_attn_wB, L0_attn_wC, L0_attn_A_log, L0_attn_W_D, L0_attn_out_w, L0_ffn_Wr, L0_ffn_W1, L0_ffn_V1, L0_ffn_W2):

    def _L0_attn_ref(resid, norm_w, skip_w, in_w, conv_w, conv_b, wd1, wd2, wd2_b, wB, wC, A_log, W_D, out_w):
        import jax, jax.numpy as jnp
        import numpy as np
        B_, L_, D_ = (2, 128, 256)
        E_, N_, R_, K_ = (512, 16, 128, 4)
        EPS = 1e-05

        def _forward(resid, norm_w, skip_w, in_w, conv_w, conv_b, wd1, wd2, wd2_b, wB, wC, A_log, W_D, out_w):
            B, L, D = resid.shape
            E, K = conv_w.shape
            N = A_log.shape[1]
            rn = resid * jax.lax.rsqrt(jnp.mean(resid * resid, -1, keepdims=True) + EPS) * norm_w
            skip = rn @ skip_w.T
            x_in = rn @ in_w.T
            xp = jnp.pad(x_in, ((0, 0), (K - 1, 0), (0, 0)))
            conv = conv_b + sum((xp[:, k:k + L, :] * conv_w[:, k] for k in range(K)))
            x = jax.nn.silu(conv)
            delta = jax.nn.softplus(x @ wd1.T @ wd2.T + wd2_b)
            A = -jnp.exp(A_log)
            Bm = x @ wB.T
            Cm = x @ wC.T

            def step(h, inp):
                d_l, b_l, c_l, x_l = inp
                h = jnp.exp(d_l[:, :, None] * A) * h + (d_l * x_l)[:, :, None] * b_l[:, None, :]
                y_l = jnp.einsum('ben,bn->be', h, c_l)
                return (h, y_l)
            h0 = jnp.zeros((B, E, N), resid.dtype)
            xs = (delta.transpose(1, 0, 2), Bm.transpose(1, 0, 2), Cm.transpose(1, 0, 2), x.transpose(1, 0, 2))
            _, ys = jax.lax.scan(step, h0, xs)
            y = ys.transpose(1, 0, 2) + x * W_D
            y = y * jax.nn.silu(skip)
            return resid + y @ out_w.T
        return _forward(resid, norm_w, skip_w, in_w, conv_w, conv_b, wd1, wd2, wd2_b, wB, wC, A_log, W_D, out_w)

    def _L0_ffn_ref(x, Wr, W1, V1, W2):
        import jax, jax.numpy as jnp
        import numpy as np
        D_MODEL = 256
        FFN_DIM = 512
        N_EXPERTS = 8
        TOP_K = 2
        orig_shape = x.shape
        xf = x.reshape(-1, x.shape[-1])
        gates = jax.nn.softmax((xf @ Wr).astype(jnp.float32), axis=-1)
        _, inds = jax.lax.top_k(-gates, TOP_K)
        inds = jax.lax.stop_gradient(inds)
        scores = jnp.take_along_axis(gates, inds, axis=-1)
        scores = scores / jnp.sum(jnp.abs(scores), axis=-1, keepdims=True)
        scores = scores.astype(x.dtype)
        onehot = jax.nn.one_hot(inds, N_EXPERTS, dtype=x.dtype)
        comb = jnp.einsum('tk,tke->te', scores, onehot)
        h = jnp.einsum('td,edf->etf', xf, W1)
        v = jnp.einsum('td,edf->etf', xf, V1)
        out = jnp.einsum('etf,efd->etd', jax.nn.silu(h) * v, W2)
        y = jnp.einsum('te,etd->td', comb, out)
        return y.reshape(orig_shape)
    x = L0_attn_resid
    xn = _layernorm(x, axis=-1)
    x = x + _L0_attn_ref(xn, L0_attn_norm_w, L0_attn_skip_w, L0_attn_in_w, L0_attn_conv_w, L0_attn_conv_b, L0_attn_wd1, L0_attn_wd2, L0_attn_wd2_b, L0_attn_wB, L0_attn_wC, L0_attn_A_log, L0_attn_W_D, L0_attn_out_w) + _L0_ffn_ref(xn, L0_ffn_Wr, L0_ffn_W1, L0_ffn_V1, L0_ffn_W2)
    return x

_drawn_inputs = setup_inputs


def setup_inputs(seed=0):
    import zlib

    import numpy as np

    out = dict(_drawn_inputs(seed))
    spreads = {'L0_attn_norm_w': (1.0, 0.2), 'L0_attn_conv_b': (0.0, 0.1), 'L0_attn_W_D': (1.0, 0.2)}
    factors = {}
    for name, (base, spread) in spreads.items():
        noise = np.random.default_rng([zlib.crc32(name.encode()), seed]).standard_normal(out[name].shape)
        drawn = base * np.exp(spread * noise) if base else spread * noise
        out[name] = jnp.asarray(drawn.astype(out[name].dtype))
    for name, factor in factors.items():
        out[name] = (out[name] * factor).astype(out[name].dtype)
    return out
```

```python
import concourse.bass as bass
from concourse import mybir
from contextlib import ExitStack

F32 = mybir.dt.float32
I32 = mybir.dt.int32
ALU = mybir.AluOpType
ACT = mybir.ActivationFunctionType
AX = mybir.AxisListType

P = 128
BATCH, SEQ, D = 4, 1024, 256
E, N, R, TAPS = 512, 16, 128, 4
EXPERTS, FF, TOPK = 8, 512, 2
EPS = 1e-5
TOKENS = BATCH * SEQ
KD, KE = D // P, E // P
CH = 256
SUB = CH // P
CHUNKS = TOKENS // CH
CPB = SEQ // CH
TT = TOKENS // P
JT = TOKENS * TOPK // P + EXPERTS
STAT_VAR, STAT_RMS, STAT_LN, STAT_LOGITS, STAT_MASK, STAT_END = 1, 9, 18, 21, 40, 58
SLOTS = JT * P
WE = KD * FF
assert WE == (FF // P) * D

F_PLACES = [1, 4, 6, 8, 10, 11, 13, 14, 16, 17, 20, 21, 22, 23, 24, 25, 26, 28]
B_PLACES = [(5, ("B1",)), (7, ("B2", 0)), (7, ("CV", 0)), (9, ("B2", 1)), (9, ("CV", 1)), (10, ("X2", 0)),
            (12, ("CV", 2)), (14, ("CV", 3)), (15, ("X2", 1)), (18, ("B3",)), (19, ("B4",)), (20, ("SP",)),
            (21, ("DL",)), (23, ("U",)), (27, ("B5",))]
O_PLACES = [(2, ("O1",)), (3, ("O2", 0)), (5, ("O2", 1)), (12, ("O3", 0)), (15, ("O3", 1))]
LAST_O = 15
FIRST_FFN, LAST_FFN = 2, 14
TPC = JT // (LAST_FFN - FIRST_FFN)
assert TPC * 3 == len(F_PLACES)


def pieces(c):
    at = [[] for _ in range(2 * N)]
    if c >= 1:
        for k, piece in O_PLACES:
            at[k].append(piece + (c - 1,) if len(piece) > 1 else (piece[0], 0, c - 1))
    if c + 1 < CHUNKS:
        for k, piece in B_PLACES:
            at[k].append(piece + (c + 1,) if len(piece) > 1 else (piece[0], 0, c + 1))
    if c == 0:
        for i in range(TT // 2 + 1):
            at[F_PLACES[i]].append(("R", i))
        at[28].append(("RA",))
        at[29].append(("RP",))
        at[30].append(("RB",))
    elif c == 1:
        for i in range(TT // 2):
            at[F_PLACES[i]].append(("D", i))
        at[29].append(("FB", -1))
    elif c < LAST_FFN:
        for k, place in enumerate(F_PLACES):
            at[place].append((("FA", "FB", "FC")[k % 3], TPC * (c - FIRST_FFN) + k // 3))
    elif c == LAST_FFN:
        at[F_PLACES[0]].append(("FA", JT))
        at[F_PLACES[1]].append(("FC", JT))
        for t in range(len(F_PLACES) - 2):
            at[F_PLACES[2 + t]].append(("S", t))
    else:
        first = len(F_PLACES) - 2
        late = [k for k in F_PLACES if k > LAST_O]
        rest = list(range(first, TT - 2))
        for t, k in zip(rest, F_PLACES[:len(rest) - len(late)] + late):
            at[k].append(("S", t))
    return at


def prologue():
    return [(p + (0,) if len(p) > 1 else (p[0], 0, 0)) for _, p in B_PLACES]


def epilogue():
    return [(p + (CHUNKS - 1,) if len(p) > 1 else (p[0], 0, CHUNKS - 1)) for _, p in O_PLACES] + \
        [("S", TT - 2), ("S", TT - 1)]


def ahead(t):
    if t == 0 or t == TT - SUB:
        return [t, t + 1]
    return [] if t + 1 in (TT - SUB, TT) else [t + 1]


def banks_of(piece):
    kind = piece[0]
    if kind == "B2":
        return ["G"] if piece[1] == 0 else ["V"]
    if kind == "O3":
        return ["H"] if piece[1] == 0 else ["V"]
    if kind == "FA":
        return (["H"] if piece[1] < JT else []) + (["G"] if piece[1] > 0 else [])
    if kind == "FB":
        return (["V"] if piece[1] >= 0 else []) + (["X"] if piece[1] + 1 < JT else [])
    if kind == "FC":
        return ["X"] if piece[1] > 0 else []
    if kind == "R":
        return ["H", "V"] if piece[1] < TT // 2 else []
    return {"B1": ["G"], "B3": ["G"], "B4": ["H", "V"], "B5": ["H", "V"], "O1": ["H", "V"], "O2": ["G"],
            "RP": ["H", "V"]}.get(kind, [])


def count_uses():
    order = list(prologue())
    begins = {}
    uses, count = {}, {"H": 0, "V": 0, "X": 0, "G": 0}

    def walk(piece):
        for b in banks_of(piece):
            uses[b, piece] = count[b]
            count[b] += 1

    for piece in order:
        walk(piece)
    for c in range(CHUNKS):
        begins[c] = dict(count)
        for place in pieces(c):
            for piece in place:
                walk(piece)
    for piece in epilogue():
        walk(piece)
    return uses, begins


def mamba_moe(nc, x, norm_w, skip_wT, in_wT, conv_w, conv_b, wd1T, wd2T, wd2_b, wBCT, A_log, W_D, out_wT,
              Wr, W1, V1, W2, ident, tri, cst, out):
    USES, BEGINS = count_uses()
    ctx = ExitStack()
    with ctx:
        def sb(name, shape, dt=F32):
            return ctx.enter_context(nc.sbuf_tensor(name, shape, dt))

        def sem(name):
            return ctx.enter_context(nc.semaphore(name))

        xbuf = nc.dram_tensor("xbuf", (SLOTS, D), F32, kind="Internal").ap()
        ybuf = nc.dram_tensor("ybuf", (SLOTS, D), F32, kind="Internal").ap()
        mbuf = nc.dram_tensor("mbuf", (TOKENS, D), F32, kind="Internal").ap()
        x_rows = x.rearrange("b l d -> (b l) d")
        out_rows = out.rearrange("b l d -> (b l) d")

        w1 = sb("w1", [P, EXPERTS * WE])
        v1 = sb("v1", [P, EXPERTS * WE])
        w2 = sb("w2", [P, EXPERTS * WE])
        inw = sb("inw", [P, KD, E])
        skw = sb("skw", [P, KD, E])
        wd1 = sb("wd1", [P, KE, R])
        wd2 = sb("wd2", [P, E])
        wbc = sb("wbc", [P, KE, 2 * N])
        outw = sb("outw", [P, KE, D])
        wrt = sb("wrt", [P, KD, EXPERTS])
        cw = sb("cw", [P, KE, TAPS])
        cb = sb("cb", [P, KE])
        db = sb("db", [P, KE])
        Am = sb("Am", [P, KE, N])
        WD = sb("WD", [P, KE])
        nw = sb("nw", [P, KD])
        idn = sb("idn", [P, P])
        edge = sb("edge", [P, KE, TAPS - 1])
        st6 = sb("st6", [P, 2, 6])
        mv = sb("mv", [P, TT, 2])
        sq = sb("sq", [P, TT])
        ta = sb("ta", [P, TT])
        rstd = sb("rstd", [P, TT])
        nmr = sb("nmr", [P, TT])
        s2 = sb("s2", [P, TT])
        nm2 = sb("nm2", [P, TT])
        r1 = sb("r1", [P, TT])
        wt1 = sb("wt1", [P, TT])
        wt2 = sb("wt2", [P, TT])
        sl1 = sb("sl1", [P, TT], I32)
        sl2 = sb("sl2", [P, TT], I32)
        te = sb("te", [1, JT], I32)
        xch = sb("xch", [P, 2, SUB, D])
        rnT = sb("rnT", [P, 2, KD, CH])
        xin = sb("xin", [P, KE, TAPS - 1 + CH])
        xc = sb("xc", [P, KE, CH])
        tap = sb("tap", [P, 2, CH])
        tqB = sb("tqB", [P, 2, CH])
        tqO = sb("tqO", [P, 2, CH])
        x2 = sb("x2", [P, 2, KE, CH])
        delta = sb("delta", [P, 2, KE, CH])
        uT = sb("uT", [P, 2, SUB, E])
        yac = sb("yac", [P, 2, SUB, E])
        y1 = sb("y1", [P, KE, CH])
        BC = sb("BC", [P, 2, SUB, 2 * N])
        dtT = sb("dtT", [P, CH])
        carry = sb("carry", [P, N, KE])
        aexp = sb("aexp", [P, 2, KE, CH])
        ub = sb("ub", [P, 2, SUB, E])
        hb = sb("hb", [P, 2, KE, CH])
        tok = sb("tok", [P, 4, D])
        xT = sb("xT", [P, 2, KD, P])
        th = sb("th", [P, FF])
        g1 = sb("g1", [P, FF])
        vs = sb("vs", [P, FF])
        gT = sb("gT", [P, FF])
        mst = sb("mst", [P, 2, D])
        xall = w1[:, :].rearrange("p (t d) -> p t d", t=TT)
        rt = v1[:, :].rearrange("p (k t e) -> p k t e", k=WE * EXPERTS // (TT * EXPERTS), t=TT)
        trim = w2[:, 0:P]
        ones = w2[:, P:2 * P]
        csts = w2[:, 2 * P:2 * P + cst.shape[1]]

        bps = [ctx.enter_context(nc.psum_tensor(f"bps{i}", [P, 512], F32)) for i in range(2)]
        hps = [ctx.enter_context(nc.psum_tensor(f"hps{i}", [P, 512], F32)) for i in range(2)]
        bank = {b: ctx.enter_context(nc.psum_tensor(f"bank{b}", [P, 512], F32)) for b in "HVXG"}

        ld_small = sem("ld_small")
        ld_x = [sem(f"ld_x{i}") for i in range(4)]
        bst = sem("bst")
        ones_set = sem("ones_set")
        ld_w = sem("ld_w")
        ld_xch = [sem("ld_xch0"), sem("ld_xch1")]
        zero_set = sem("zero_set")
        zeroed = sem("zeroed")
        wprep = sem("wprep")
        aprep = sem("aprep")
        stat = sem("stat")
        sact = sem("sact")
        full = {b: sem("full_" + b) for b in "HVXG"}
        free = {b: sem("free_" + b) for b in "HVXG"}
        z_done = sem("z_done")
        halo = sem("halo")
        conv = sem("conv")
        cvs = sem("cvs")
        tqb = sem("tqb")
        x2r = sem("x2r")
        dtr = sem("dtr")
        spx = sem("spx")
        dlt = sem("dlt")
        uu = sem("uu")
        tqo = sem("tqo")
        gate = sem("gate")
        m_out = [sem("m_out0"), sem("m_out1")]
        s_ub = sem("s_ub")
        s_bT = sem("s_bT")
        s_a = sem("s_a")
        s_scan = sem("s_scan")
        s_cc = sem("s_cc")
        s_hT = sem("s_hT")
        s_acc = sem("s_acc")
        xn_r = sem("xn_r")
        xTr = sem("xTr")
        lgt = sem("lgt")
        disp = [sem(f"disp{i}") for i in range(4)]
        ld_xs = [sem("ld_xs0"), sem("ld_xs1")]
        s_th = sem("s_th")
        s_g = sem("s_g")
        y_out = [sem("y_out0"), sem("y_out1")]
        gat = [sem(f"gat{i}") for i in range(2)]
        ld_s = [sem("ld_s0"), sem("ld_s1")]
        sums = sem("sums")
        o_out = [sem("o_out0"), sem("o_out1")]
        block = ctx.enter_context(nc.Block())

        gbuf = [g1[:, :], vs[:, :]]
        sbuf_x = [tok[:, 0, :], tok[:, 1, :]]
        sbuf_m = [tok[:, 2, :], tok[:, 3, :]]

        def at_least(eng, s, value):
            if value > 0:
                eng.wait_ge(s, value)

        def wait_full(eng, b, piece):
            at_least(eng, full[b], USES[b, piece] + 1)

        def wait_free(eng, b, piece):
            at_least(eng, free[b], USES[b, piece])

        def wait_taken(eng, b, piece):
            at_least(eng, free[b], USES[b, piece] + 1)

        NSMALL = 18

        @block.sync
        def _(sp):
            for t in range(0, TT, 8):
                sp.dma_start(xall[:, t:t + 8, :], x_rows[t * P:(t + 8) * P, :].rearrange("(t p) d -> p t d", p=P)).then_inc(ld_x[t // 8], 16)

            def load_chunk(c):
                if c >= 2:
                    wait_full(sp, "G", ("B1", 0, c - 2))
                sp.dma_start(xch[:, c % 2, :, :], x_rows[c * CH:(c + 1) * CH, :].rearrange("(s p) d -> p s d", p=P)).then_inc(ld_xch[c % 2], 16)

            def load_tile(j):
                if j >= 2:
                    wait_full(sp, "X", ("FB", j - 3))
                sp.dma_start(tok[:, j % 2, :], xbuf[j * P:(j + 1) * P, :]).then_inc(ld_xs[j % 2], 16)

            def do(piece):
                kind = piece[0]
                if kind == "B1" and piece[2] + 1 < CHUNKS:
                    load_chunk(piece[2] + 1)
                elif kind == "O3":
                    s, c = piece[1], piece[2]
                    wait_taken(sp, "HV"[s], piece)
                    t = SUB * c + s
                    sp.dma_start(mbuf[t * P:(t + 1) * P, :], mst[:, s, :]).then_inc(m_out[s], 16)
                elif kind == "D" and piece[1] == TT // 2 - 1:
                    sp.wait_ge(xn_r, 2 * TT)
                    sp.dma_start(w1[:, :].rearrange("p (e k f) -> p e k f", e=EXPERTS, k=KD), W1.rearrange("e (k p) f -> p e k f", p=P)).then_inc(ld_w, 16)
                elif kind == "RB":
                    sp.wait_ge(stat, STAT_END)
                    sp.dma_start(v1[:, :].rearrange("p (e k f) -> p e k f", e=EXPERTS, k=KD), V1.rearrange("e (k p) f -> p e k f", p=P)).then_inc(ld_w, 16)
                    sp.dma_start(w2[:, :].rearrange("p (e k f) -> p e k f", e=EXPERTS, k=FF // P), W2.rearrange("e (k p) f -> p e k f", p=P)).then_inc(ld_w, 16)
                elif kind == "FB" and piece[1] == -1:
                    for i in range(4):
                        sp.wait_ge(disp[i], 16 * 2 * TT // 4)
                    load_tile(0)
                    load_tile(1)
                elif kind == "FA" and piece[1] + 2 < JT:
                    load_tile(piece[1] + 2)
                elif kind == "FC" and piece[1] > 0:
                    j = piece[1] - 1
                    wait_taken(sp, "X", piece)
                    sp.dma_start(ybuf[j * P:(j + 1) * P, :], tok[:, 2 + j % 2, :]).then_inc(y_out[j % 2], 16)
                elif kind == "S":
                    t = piece[1]
                    if t == 0:
                        for k in range(2):
                            sp.wait_ge(y_out[k], 16 * JT // 2)
                    for tn in ahead(t):
                        i = tn % 2
                        sp.wait_ge(m_out[i], 16 * (tn // 2 + 1))
                        at_least(sp, o_out[i], 16 * (tn // 2))
                        sp.dma_start(sbuf_x[i], x_rows[tn * P:(tn + 1) * P, :]).then_inc(ld_s[i], 16)
                        sp.dma_start(sbuf_m[i], mbuf[tn * P:(tn + 1) * P, :]).then_inc(ld_s[i], 16)
                    sp.wait_ge(sums, 3 * (t + 1))
                    sp.dma_start(out_rows[t * P:(t + 1) * P, :], sbuf_m[t % 2]).then_inc(o_out[t % 2], 16)

            load_chunk(0)
            for piece in prologue():
                do(piece)
            for c in range(CHUNKS):
                for place in pieces(c):
                    for piece in place:
                        do(piece)
            for piece in epilogue():
                do(piece)
            for i in range(2):
                sp.wait_ge(o_out[i], 16 * TT // 2)
                sp.wait_ge(m_out[i], 16 * TT // 2)
                sp.wait_ge(y_out[i], 16 * JT // 2)

        @block.scalar
        def _(act):
            for dst, src in [
                (idn[:, :], ident), (trim, tri), (csts, cst),
                (inw[:, :, :], in_wT.rearrange("(k p) e -> p k e", p=P)),
                (skw[:, :, :], skip_wT.rearrange("(k p) e -> p k e", p=P)),
                (wd1[:, :, :], wd1T.rearrange("(k p) r -> p k r", p=P)),
                (wd2[:, :], wd2T),
                (wbc[:, :, 0:N], wBCT[0].rearrange("(k p) n -> p k n", p=P)),
                (wbc[:, :, N:2 * N], wBCT[1].rearrange("(k p) n -> p k n", p=P)),
                (outw[:, :, :], out_wT.rearrange("(k p) d -> p k d", p=P)),
                (wrt[:, :, :], Wr.rearrange("(k p) e -> p k e", p=P)),
                (cw[:, :, :], conv_w.rearrange("(k p) w -> p k w", p=P)),
                (cb[:, :], conv_b),
                (db[:, :], wd2_b),
                (Am[:, :, :], A_log.rearrange("(k p) n -> p k n", p=P)),
                (WD[:, :], W_D),
                (nw[:, :], norm_w),
            ]:
                act.dma_start(dst, src).then_inc(ld_small, 16)
            act.wait_ge(zero_set, 2)
            act.dma_start(xbuf.rearrange("(p a) d -> p a d", p=P),
                          gT[:, 0:D].unsqueeze(1).to_broadcast([P, JT, D])).then_inc(zeroed, 16)
            act.wait_ge(ld_small, 16 * (NSMALL - 1))
            nc.scalar.activation(Am[:, :, :], Am[:, :, :], ACT.Exp).then_inc(aprep, 1)
            act.wait_ge(stat, STAT_VAR)
            nc.scalar.activation(sq[:, :], ta[:, :], ACT.Sqrt).then_inc(sact, 1)
            act.wait_ge(stat, STAT_RMS)
            nc.scalar.activation(sq[:, :], ta[:, :], ACT.Sqrt).then_inc(sact, 1)
            act.wait_ge(stat, STAT_LN)
            act.wait_ge(wprep, 6)

            def exps(u):
                c, n = divmod(u, N)
                if n == 0:
                    act.wait_ge(dlt, c + 1)
                for e in range(KE):
                    at_least(act, s_scan, 4 * (u - 2) + e + 1)
                    nc.scalar.activation(aexp[:, u % 2, e, :], delta[:, c % 2, e, :], ACT.Exp,
                                         scale=Am[:, e, n:n + 1]).then_inc(s_a, 1)

            def do(piece):
                kind = piece[0]
                if kind == "B1":
                    c = piece[2]
                    act.wait_ge(ld_xch[c % 2], 16 * (c // 2 + 1))
                    for s in range(SUB):
                        t = SUB * c + s
                        nc.scalar.activation(xch[:, c % 2, s, :], xch[:, c % 2, s, :], ACT.Identity,
                                             bias=nm2[:, t:t + 1], scale=s2[:, t:t + 1]).then_inc(z_done, 1)
                    wait_full(act, "G", piece)
                    if c >= 2:
                        wait_full(act, "G", ("O2", 1, c - 2))
                    for k in range(KD):
                        ins = nc.scalar.activation(rnT[:, c % 2, k, :], bank["G"][:, k * CH:(k + 1) * CH], ACT.Identity,
                                                   scale=nw[:, k:k + 1])
                    ins.then_inc(free["G"], 1)
                elif kind == "B2":
                    q, c = piece[1], piece[2]
                    b = "G" if q == 0 else "V"
                    at_least(act, conv, KE * c)
                    if q == 0:
                        if c % CPB == 0:
                            src = edge[:, :, :]
                        else:
                            src = xin[:, :, CH:CH + TAPS - 1]
                        nc.scalar.activation(xin[:, :, 0:TAPS - 1], src, ACT.Copy).then_inc(halo, 1)
                    act.wait_ge(halo, c + 1)
                    wait_full(act, b, piece)
                    nc.scalar.activation(xin[:, 2 * q:2 * q + 2, TAPS - 1:], bank[b][:, :].rearrange("p (k t) -> p k t", k=2),
                                         ACT.Copy).then_inc(free[b], 1)
                elif kind == "X2":
                    q, c = piece[1], piece[2]
                    act.wait_ge(conv, KE * c + 2 * q + 2)
                    at_least(act, x2r, 2 * c + q)
                    nc.scalar.activation(tqB[:, :, :], xc[:, 2 * q:2 * q + 2, :], ACT.Tanh, scale=0.5).then_inc(tqb, 1)
                elif kind == "B3":
                    c = piece[2]
                    wait_full(act, "G", piece)
                    at_least(act, s_ub, 2 * N * (c - 1))
                    at_least(act, s_acc, 2 * N * (c - 1))
                    if c >= 1:
                        wait_full(act, "V", ("B4", 0, c - 1))
                    nc.scalar.activation(dtT[:, :], bank["G"][:, 0:CH], ACT.Copy)
                    nc.scalar.activation(BC[:, c % 2, :, :], bank["G"][:, CH:CH + SUB * 2 * N].rearrange("p (s n) -> p s n", s=SUB),
                                         ACT.Copy).then_inc(free["G"], 1)
                elif kind == "B4":
                    c = piece[2]
                    if c >= 1:
                        at_least(act, dlt, c)
                    if c >= 2:
                        wait_full(act, "V", ("O3", 1, c - 2))
                        act.wait_ge(uu, c - 1)
                    for q, b in enumerate("HV"):
                        wait_full(act, b, piece)
                        for i in range(2):
                            e = 2 * q + i
                            nc.scalar.activation(y1[:, e, :], bank[b][:, i * CH:(i + 1) * CH], ACT.Abs,
                                                 bias=db[:, e:e + 1]).then_inc(spx, 1)
                            ins = nc.scalar.activation(delta[:, c % 2, e, :], bank[b][:, i * CH:(i + 1) * CH], ACT.Relu,
                                                       bias=db[:, e:e + 1])
                        ins.then_inc(free[b], 1)
                elif kind == "SP":
                    c = piece[2]
                    act.wait_ge(spx, 6 * c + 4)
                    nc.scalar.activation(y1[:, :, :], y1[:, :, :], ACT.Exp, scale=-1.0).then_inc(spx, 1)
                    act.wait_ge(spx, 6 * c + 5)
                    nc.scalar.activation(y1[:, :, :], y1[:, :, :], ACT.Ln, bias=1.0).then_inc(spx, 1)
                elif kind == "B5":
                    c = piece[2]
                    at_least(act, s_ub, 2 * N * (c - 1))
                    for s, b in enumerate("HV"):
                        wait_full(act, b, piece)
                        nc.scalar.activation(uT[:, c % 2, s, :], bank[b][:, :], ACT.Copy).then_inc(free[b], 1)
                elif kind == "O2":
                    q, c = piece[1], piece[2]
                    wait_full(act, "G", piece)
                    at_least(act, gate, 2 * c + q)
                    nc.scalar.activation(tqO[:, :, :], bank["G"][:, :].rearrange("p (k t) -> p k t", k=2), ACT.Tanh,
                                         scale=0.5).then_inc(tqo, 1)
                elif kind == "O3":
                    s, c = piece[1], piece[2]
                    b = "HV"[s]
                    t = SUB * c + s
                    wait_full(act, b, piece)
                    at_least(act, m_out[s], 16 * c)
                    nc.scalar.activation(mst[:, s, :], bank[b][:, 0:D], ACT.Identity, bias=nmr[:, t:t + 1]).then_inc(free[b], 1)
                elif kind == "R":
                    i = piece[1]
                    if i < TT // 2:
                        if i >= 2:
                            wait_full(act, "V", ("R", i - 2))
                        for t in (2 * i, 2 * i + 1):
                            nc.scalar.activation(tok[:, t % 4, :], xall[:, t, :], ACT.Identity, bias=nmr[:, t:t + 1],
                                                 scale=rstd[:, t:t + 1]).then_inc(xn_r, 1)
                        for k, t in enumerate((2 * i, 2 * i + 1)):
                            wait_full(act, "HV"[k], piece)
                            at_least(act, lgt, t - 1)
                            nc.scalar.activation(xT[:, k, :, :], bank["HV"[k]][:, 0:D].rearrange("p (k t) -> p k t", k=KD),
                                                 ACT.Copy).then_inc(free["HV"[k]], 1)
                elif kind == "RA":
                    act.wait_ge(stat, STAT_LOGITS)
                    nc.scalar.activation(rt[:, 1], rt[:, 0], ACT.Exp).then_inc(sact, 1)
                elif kind == "D":
                    for t in (2 * piece[1], 2 * piece[1] + 1):
                        if t < 4:
                            wait_full(act, "V", ("R", TT // 2 - 1))
                        else:
                            act.wait_ge(disp[t % 4], 16 * 2 * (t // 4))
                        nc.scalar.activation(tok[:, t % 4, :], xall[:, t, :], ACT.Identity, bias=nmr[:, t:t + 1],
                                             scale=rstd[:, t:t + 1]).then_inc(xn_r, 1)
                elif kind == "FA":
                    j = piece[1]
                    if j > 0:
                        wait_full(act, "G", piece)
                    if j < JT:
                        wait_full(act, "H", piece)
                        nc.scalar.activation(th[:, :], bank["H"][:, :], ACT.Tanh, scale=0.5).then_inc(s_th, 1)
                    if j > 0:
                        if j > 1:
                            wait_full(act, "X", ("FC", j - 1))
                        nc.scalar.activation(gT[:, :], bank["G"][:, :], ACT.Copy).then_inc(free["G"], 1)
                elif kind == "FB":
                    j = piece[1]
                    if j >= 0:
                        wait_full(act, "V", piece)
                        at_least(act, s_g, j)
                        nc.scalar.activation(vs[:, :], bank["V"][:, :], ACT.Copy).then_inc(free["V"], 1)
                    if j + 1 < JT:
                        wait_full(act, "X", piece)
                        if j < 0:
                            act.wait_ge(lgt, TT)
                        nc.scalar.activation(xT[:, (j + 1) % 2, :, :], bank["X"][:, 0:D].rearrange("p (k t) -> p k t", k=KD),
                                             ACT.Copy).then_inc(free["X"], 1)
                elif kind == "FC" and piece[1] > 0:
                    j = piece[1] - 1
                    wait_full(act, "X", piece)
                    if j < 2:
                        act.wait_ge(disp[2 + j % 2], 16 * 2 * TT // 4)
                    else:
                        act.wait_ge(y_out[j % 2], 16 * (j // 2))
                    nc.scalar.activation(tok[:, 2 + j % 2, :], bank["X"][:, 0:D], ACT.Copy).then_inc(free["X"], 1)

            for piece in prologue():
                do(piece)
            exps(0)
            for c in range(CHUNKS):
                at = pieces(c)
                for n in range(N):
                    if N * c + n + 1 < N * CHUNKS:
                        exps(N * c + n + 1)
                    for piece in at[2 * n] + at[2 * n + 1]:
                        do(piece)
            for piece in epilogue():
                do(piece)

        @block.gpsimd
        def _(pool):
            nc.gpsimd.memset(gT[:, :], 0.0).then_inc(zero_set, 1)
            nc.gpsimd.memset(edge[:, :, :], 0.0).then_inc(zero_set, 1)
            pool.wait_ge(ld_small, 16 * (NSMALL - 1))
            for w, k in ((wd1[:, :, :], 0.5), (wbc[:, :, 0:N], 0.25), (wbc[:, :, N:2 * N], 0.5), (WD[:, :], 0.5),
                         (outw[:, :, :], 0.5)):
                nc.gpsimd.tensor_scalar(w, w, k, 1.0, ALU.mult, ALU.mult).then_inc(wprep, 1)
            pool.wait_ge(aprep, 1)
            nc.gpsimd.tensor_scalar(Am[:, :, :], Am[:, :, :], -1.0, 1.0, ALU.mult, ALU.mult).then_inc(wprep, 1)
            pool.wait_ge(wprep, 6)
            def products(u):
                c, n = divmod(u, N)
                if n == 0:
                    wait_taken(pool, "V", ("B5", 0, c))
                at_least(pool, s_bT, 2 * (u - 1))
                for s in range(SUB):
                    nc.gpsimd.tensor_scalar(ub[:, u % 2, s, :], uT[:, c % 2, s, :], BC[:, c % 2, s, n:n + 1], 1.0,
                                            ALU.mult, ALU.mult).then_inc(s_ub, 1)

            def do(piece):
                kind = piece[0]
                if kind == "CV":
                    e, c = piece[1], piece[2]
                    b = "G" if e < 2 else "V"
                    wait_taken(pool, b, ("B2", e // 2, c))
                    if c >= 1:
                        wait_full(pool, "V", ("B5", 0, c - 1))
                    first = 6 * (KE * c + e)

                    def product(dst, w, add):
                        return nc.gpsimd.tensor_scalar(dst, xin[:, e, w:w + CH], cw[:, e, w:w + 1], add,
                                                       ALU.mult, ALU.mult if w else ALU.add)

                    product(xc[:, e, :], 0, cb[:, e:e + 1]).then_inc(cvs, 1)
                    product(tap[:, 0, :], 1, 1.0).then_inc(cvs, 1)
                    product(tap[:, 1, :], 2, 1.0).then_inc(cvs, 1)
                    pool.wait_ge(cvs, first + 3)
                    nc.gpsimd.tensor_tensor(xc[:, e, :], xc[:, e, :], tap[:, 0, :], ALU.add).then_inc(cvs, 1)
                    pool.wait_ge(cvs, first + 4)
                    product(tap[:, 0, :], 3, 1.0).then_inc(cvs, 1)
                    nc.gpsimd.tensor_tensor(xc[:, e, :], xc[:, e, :], tap[:, 1, :], ALU.add).then_inc(cvs, 1)
                    pool.wait_ge(cvs, first + 6)
                    nc.gpsimd.tensor_tensor(xc[:, e, :], xc[:, e, :], tap[:, 0, :], ALU.add).then_inc(conv, 1)
                    pool.wait_ge(conv, KE * c + e + 1)
                elif kind == "DL":
                    c = piece[2]
                    pool.wait_ge(spx, 6 * c + 6)
                    wait_taken(pool, "V", ("B4", 0, c))
                    nc.gpsimd.tensor_tensor(delta[:, c % 2, :, :], delta[:, c % 2, :, :], y1[:, :, :], ALU.add).then_inc(dlt, 1)
                elif kind == "U":
                    c = piece[2]
                    pool.wait_ge(dlt, c + 1)
                    pool.wait_ge(x2r, 2 * c + 2)
                    nc.gpsimd.tensor_tensor(xc[:, :, :], delta[:, c % 2, :, :], x2[:, c % 2, :, :], ALU.mult).then_inc(uu, 1)
                elif kind == "O2":
                    q, c = piece[1], piece[2]
                    wait_taken(pool, "G", piece)
                    wait_taken(pool, "HV"[q], ("O1", 0, c))
                    nc.gpsimd.tensor_tensor(y1[:, 2 * q:2 * q + 2, :], y1[:, 2 * q:2 * q + 2, :], tqO[:, :, :],
                                            ALU.mult).then_inc(gate, 1)
                elif kind == "D":
                    if piece[1] == 0:
                        pool.wait_ge(zeroed, 16)
                        pool.wait_ge(stat, STAT_END)
                    for t in (2 * piece[1], 2 * piece[1] + 1):
                        pool.wait_ge(xn_r, TT + t + 1)
                        for sl in (sl1, sl2):
                            nc.gpsimd.indirect_dma_start(
                                out=xbuf, out_offset=bass.IndirectOffsetOnAxis(ap=sl[:, t:t + 1], axis=0),
                                in_=tok[:, t % 4, :], in_offset=None).then_inc(disp[t % 4], 16)
                elif kind == "FB" and piece[1] >= 0:
                    j = piece[1]
                    wait_taken(pool, "V", piece)
                    wait_taken(pool, "H", ("FA", j))
                    nc.gpsimd.tensor_tensor(th[:, :], g1[:, :], vs[:, :], ALU.mult).then_inc(s_g, 1)
                elif kind == "S":
                    t = piece[1]
                    if t == 0:
                        for k in range(2):
                            pool.wait_ge(y_out[k], 16 * JT // 2)
                    for tn in ahead(t):
                        at_least(pool, sums, 3 * (tn - 1))
                        for k, sl in enumerate((sl1, sl2)):
                            nc.gpsimd.indirect_dma_start(
                                out=gbuf[tn % 2][:, k * D:(k + 1) * D], out_offset=None, in_=ybuf,
                                in_offset=bass.IndirectOffsetOnAxis(ap=sl[:, tn:tn + 1], axis=0)).then_inc(gat[tn % 2], 16)

            for piece in prologue():
                do(piece)
            products(0)
            for c in range(CHUNKS):
                at = pieces(c)
                for n in range(N):
                    u = N * c + n
                    if u + 1 < N * CHUNKS:
                        products(u + 1)
                    for piece in at[2 * n]:
                        do(piece)
                    pool.wait_ge(s_scan, 4 * u + 4)
                    nc.gpsimd.tensor_copy(carry[:, n, :], hb[:, u % 2, :, CH - 1]).then_inc(s_cc, 1)
                    for piece in at[2 * n + 1]:
                        do(piece)
            for piece in epilogue():
                do(piece)

        @block.tensor
        def _(pe):
            pe.wait_ge(ld_small, 16 * (NSMALL - 1))
            pe.wait_ge(wprep, 6)

            def turn_products(u):
                pe.wait_ge(s_ub, 2 * u + 2)
                for q in range(2):
                    at_least(pe, s_scan, 4 * (u - 1) + 2 * q + 2)
                    for s in range(SUB):
                        for i in range(2):
                            e = 2 * q + i
                            mm = pe.transpose(bps[q][:, i * CH + s * P:i * CH + (s + 1) * P],
                                              ub[:, u % 2, s, e * P:(e + 1) * P], idn[:, :])
                    mm.then_inc(s_bT, 1)

            def turn_states(u):
                pe.wait_ge(s_scan, 4 * u + 4)
                for s in range(SUB):
                    at_least(pe, s_acc, 2 * (u - 1) + s + 1)
                    for e in range(KE):
                        mm = pe.transpose(hps[s][:, e * P:(e + 1) * P], hb[:, u % 2, e, s * P:(s + 1) * P], idn[:, :])
                    mm.then_inc(s_hT, 1)

            def do(piece):
                kind = piece[0]
                if kind == "B1":
                    c = piece[2]
                    wait_free(pe, "G", piece)
                    for s in range(SUB):
                        pe.wait_ge(z_done, SUB * c + s + 1)
                        for k in range(KD):
                            mm = pe.transpose(bank["G"][:, k * CH + s * P:k * CH + (s + 1) * P],
                                              xch[:, c % 2, s, k * P:(k + 1) * P], idn[:, :])
                    mm.then_inc(full["G"], 1)
                elif kind == "B2" or kind == "O2":
                    q, c = piece[1], piece[2]
                    b = "G" if q == 0 or kind == "O2" else "V"
                    w = inw if kind == "B2" else skw
                    wait_free(pe, b, piece)
                    wait_taken(pe, "G", ("B1", 0, c))
                    for i in range(2):
                        e = 2 * q + i
                        for k in range(KD):
                            mm = pe.matmul(bank[b][:, i * CH:(i + 1) * CH], w[:, k, e * P:(e + 1) * P],
                                           rnT[:, c % 2, k, :], start=(k == 0), stop=(k == KD - 1))
                    mm.then_inc(full[b], 1)
                elif kind == "B3":
                    c = piece[2]
                    wait_free(pe, "G", piece)
                    pe.wait_ge(x2r, 2 * c + 2)
                    for k in range(KE):
                        pe.matmul(bank["G"][:, 0:CH], wd1[:, k, :], x2[:, c % 2, k, :], start=(k == 0), stop=(k == KE - 1))
                    for s in range(SUB):
                        for k in range(KE):
                            mm = pe.matmul(bank["G"][:, CH + s * 2 * N:CH + (s + 1) * 2 * N], x2[:, c % 2, k, s * P:(s + 1) * P],
                                           wbc[:, k, :], start=(k == 0), stop=(k == KE - 1))
                    mm.then_inc(full["G"], 1)
                elif kind == "B4":
                    c = piece[2]
                    wait_taken(pe, "G", ("B3", 0, c))
                    for q, b in enumerate("HV"):
                        wait_free(pe, b, piece)
                        for i in range(2):
                            e = 2 * q + i
                            mm = pe.matmul(bank[b][:, i * CH:(i + 1) * CH], wd2[:, e * P:(e + 1) * P], dtT[:, :],
                                           start=True, stop=True)
                        mm.then_inc(full[b], 1)
                elif kind == "B5":
                    c = piece[2]
                    pe.wait_ge(uu, c + 1)
                    for s, b in enumerate("HV"):
                        wait_free(pe, b, piece)
                        for e in range(KE):
                            mm = pe.transpose(bank[b][:, e * P:(e + 1) * P], xc[:, e, s * P:(s + 1) * P], idn[:, :])
                        mm.then_inc(full[b], 1)
                elif kind == "O1":
                    c = piece[2]
                    pe.wait_ge(s_acc, 2 * N * (c + 1))
                    for q, b in enumerate("HV"):
                        wait_free(pe, b, piece)
                        for s in range(SUB):
                            for i in range(2):
                                e = 2 * q + i
                                mm = pe.transpose(bank[b][:, i * CH + s * P:i * CH + (s + 1) * P],
                                                  yac[:, c % 2, s, e * P:(e + 1) * P], idn[:, :])
                        mm.then_inc(full[b], 1)
                elif kind == "O3":
                    s, c = piece[1], piece[2]
                    b = "HV"[s]
                    wait_free(pe, b, piece)
                    pe.wait_ge(gate, 2 * c + 2)
                    for k in range(KE):
                        mm = pe.matmul(bank[b][:, 0:D], y1[:, k, s * P:(s + 1) * P], outw[:, k, :],
                                       start=(k == 0), stop=(k == KE - 1))
                    mm.then_inc(full[b], 1)
                elif kind == "R":
                    i = piece[1]
                    if i > 0:
                        for k, t in enumerate((2 * i - 2, 2 * i - 1)):
                            wait_taken(pe, "HV"[k], ("R", i - 1))
                            for kd in range(KD):
                                mm = pe.matmul(bank["X"][:, t * EXPERTS:(t + 1) * EXPERTS], xT[:, k, kd, :], wrt[:, kd, :],
                                               start=(kd == 0), stop=(kd == KD - 1))
                            mm.then_inc(lgt, 1)
                    if i < TT // 2:
                        for k, t in enumerate((2 * i, 2 * i + 1)):
                            wait_free(pe, "HV"[k], piece)
                            pe.wait_ge(xn_r, t + 1)
                            for kd in range(KD):
                                mm = pe.transpose(bank["HV"[k]][:, kd * P:(kd + 1) * P], tok[:, t % 4, kd * P:(kd + 1) * P], idn[:, :])
                            mm.then_inc(full["HV"[k]], 1)
                elif kind == "RP":
                    pe.wait_ge(stat, STAT_MASK)
                    pe.wait_ge(ones_set, 1)
                    for b, w in (("H", trim), ("V", ones)):
                        wait_free(pe, b, piece)
                        pe.matmul(bank[b][:, 0:TT * EXPERTS], w, rt[:, 7].rearrange("p t e -> p (t e)"), start=True, stop=True).then_inc(full[b], 1)
                elif kind == "FA":
                    j = piece[1]
                    if j < JT:
                        if j == 0:
                            pe.wait_ge(ld_w, 48)
                        col = pe.value_load(te[0:1, j:j + 1], min_val=0, max_val=(EXPERTS - 1) * WE)
                        first_col[0] = col
                        wait_taken(pe, "X", ("FB", j - 1))
                        wait_free(pe, "H", piece)
                        for k in range(KD):
                            mm = pe.matmul(bank["H"][:, :], xT[:, j % 2, k, :], w1[:, bass.ds(col + k * FF, FF)],
                                           start=(k == 0), stop=(k == KD - 1))
                        mm.then_inc(full["H"], 1)
                    if j > 0:
                        wait_free(pe, "G", piece)
                        pe.wait_ge(s_g, j)
                        for k in range(FF // P):
                            mm = pe.transpose(bank["G"][:, k * P:(k + 1) * P], th[:, k * P:(k + 1) * P], idn[:, :])
                        mm.then_inc(full["G"], 1)
                elif kind == "FB":
                    j = piece[1]
                    if j >= 0:
                        wait_free(pe, "V", piece)
                        for k in range(KD):
                            mm = pe.matmul(bank["V"][:, :], xT[:, j % 2, k, :], v1[:, bass.ds(first_col[0] + k * FF, FF)],
                                           start=(k == 0), stop=(k == KD - 1))
                        mm.then_inc(full["V"], 1)
                    if j + 1 < JT:
                        if j < 0:
                            pe.wait_ge(lgt, TT)
                        pe.wait_ge(ld_xs[(j + 1) % 2], 16 * ((j + 1) // 2 + 1))
                        wait_free(pe, "X", piece)
                        for k in range(KD):
                            mm = pe.transpose(bank["X"][:, k * P:(k + 1) * P], tok[:, (j + 1) % 2, k * P:(k + 1) * P], idn[:, :])
                        mm.then_inc(full["X"], 1)
                elif kind == "FC" and piece[1] > 0:
                    j = piece[1] - 1
                    col = pe.value_load(te[0:1, j:j + 1], min_val=0, max_val=(EXPERTS - 1) * WE)
                    wait_taken(pe, "G", ("FA", j + 1))
                    wait_free(pe, "X", piece)
                    for k in range(FF // P):
                        mm = pe.matmul(bank["X"][:, 0:D], gT[:, k * P:(k + 1) * P], w2[:, bass.ds(col + k * D, D)],
                                       start=(k == 0), stop=(k == FF // P - 1))
                    mm.then_inc(full["X"], 1)

            first_col = [None]
            for piece in prologue():
                do(piece)
            for c in range(CHUNKS):
                at = pieces(c)
                for n in range(N):
                    u = N * c + n
                    turn_products(u)
                    for piece in at[2 * n]:
                        do(piece)
                    if u >= 1:
                        turn_states(u - 1)
                    for piece in at[2 * n + 1]:
                        do(piece)
            turn_states(N * CHUNKS - 1)
            for piece in epilogue():
                do(piece)

        @block.vector
        def _(dve):
            done = [0]

            def link(ins):
                done[0] += 1
                ins.then_inc(stat, 1)
                dve.wait_ge(stat, done[0])

            v = nc.vector
            v.memset(ones, 1.0).then_inc(ones_set, 1)
            for t in range(TT):
                if t % 8 == 0:
                    dve.wait_ge(ld_x[t // 8], 16)
                if t >= 2:
                    dve.wait_ge(bst, 2 * t - 2)
                v.bn_stats(st6[:, t % 2, :], xall[:, t, :]).then_inc(bst, 1)
                dve.wait_ge(bst, 2 * t + 1)
                v.bn_aggr(mv[:, t, :], st6[:, t % 2, :]).then_inc(bst, 1)
            dve.wait_ge(bst, 2 * TT)
            mean, var = mv[:, :, 0], mv[:, :, 1]

            def inverse_root(dst):
                link(v.reciprocal(dst, sq[:, :]))
                link(v.tensor_tensor(sq[:, :], dst, dst, ALU.mult))
                link(v.tensor_tensor(sq[:, :], sq[:, :], ta[:, :], ALU.mult))
                link(v.tensor_scalar(sq[:, :], sq[:, :], -0.5, 1.5, ALU.mult, ALU.add))
                link(v.tensor_tensor(dst, dst, sq[:, :], ALU.mult))

            link(v.tensor_scalar(ta[:, :], var, EPS, None, ALU.add))
            dve.wait_ge(sact, 1)
            inverse_root(rstd[:, :])
            link(v.tensor_tensor(r1[:, :], rstd[:, :], rstd[:, :], ALU.mult))
            link(v.tensor_tensor(r1[:, :], r1[:, :], var, ALU.mult))
            link(v.tensor_scalar(ta[:, :], r1[:, :], EPS, None, ALU.add))
            assert done[0] == STAT_RMS
            dve.wait_ge(sact, 2)
            inverse_root(s2[:, :])
            link(v.tensor_tensor(s2[:, :], s2[:, :], rstd[:, :], ALU.mult))
            link(v.scalar_tensor_tensor(out=nmr[:, :], in0=mean, scalar=-1.0, in1=rstd[:, :], op0=ALU.mult, op1=ALU.mult))
            link(v.scalar_tensor_tensor(out=nm2[:, :], in0=mean, scalar=-1.0, in1=s2[:, :], op0=ALU.mult, op1=ALU.mult))
            link(v.tensor_scalar(r1[:, :], rstd[:, :], 1.0, None, ALU.add))
            assert done[0] == STAT_LN

            def scans(u):
                c, n = divmod(u, N)
                at_least(dve, s_hT, 2 * (u - 1))
                at_least(dve, s_cc, u - 1)
                for e in range(KE):
                    dve.wait_ge(s_a, 4 * u + e + 1)
                    if e % 2 == 0:
                        dve.wait_ge(s_bT, 2 * u + e // 2 + 1)
                    first = 0.0 if c % CPB == 0 else carry[:, n, e:e + 1]
                    v.tensor_tensor_scan(hb[:, u % 2, e, :], aexp[:, u % 2, e, :], bps[e // 2][:, (e % 2) * CH:(e % 2 + 1) * CH],
                                         first, ALU.mult, ALU.add).then_inc(s_scan, 1)

            def sum_states(u):
                c, n = divmod(u, N)
                if n == 0 and c >= 2:
                    wait_full(dve, "V", ("O1", 0, c - 2))
                for s in range(SUB):
                    dve.wait_ge(s_hT, 2 * u + s + 1)
                    at_least(dve, s_acc, 2 * (u - 1) + s + 1)
                    scale = BC[:, c % 2, s, N + n:N + n + 1]
                    if n == 0:
                        ins = v.tensor_scalar(yac[:, c % 2, s, :], hps[s][:, :], scale, None, ALU.mult)
                    else:
                        ins = v.scalar_tensor_tensor(out=yac[:, c % 2, s, :], in0=hps[s][:, :], scalar=scale,
                                                     in1=yac[:, c % 2, s, :], op0=ALU.mult, op1=ALU.add)
                    ins.then_inc(s_acc, 1)

            def router_choice():
                lg, gt, eq, cand, oh1, gt2, oh2, msk = (rt[:, k] for k in range(8))
                small = [rt[:, 8 + k].rearrange("p t e -> p (t e)")[:, 0:TT] for k in range(4)]
                m1, m2, id1, den = small
                wide = lambda a: a.unsqueeze(2).to_broadcast([P, TT, EXPERTS])
                eid = csts[:, 0:TT * EXPERTS].rearrange("p (t e) -> p t e", t=TT)
                dve.wait_ge(lgt, TT)
                link(v.tensor_copy(lg, bank["X"][:, 0:TT * EXPERTS].rearrange("p (t e) -> p t e", t=TT)))
                link(v.tensor_reduce(m1, lg, AX.X, ALU.max))
                link(v.tensor_tensor(lg, lg, wide(m1), ALU.subtract))
                assert done[0] == STAT_LOGITS, done
                dve.wait_ge(sact, 3)
                link(v.tensor_reduce(den, gt, AX.X, ALU.add))
                link(v.reciprocal(den, den))
                link(v.tensor_tensor(gt, gt, wide(den), ALU.mult))
                for src, m, oh in ((gt, m1, oh1), (gt2, m2, oh2)):
                    link(v.tensor_reduce(m, src, AX.X, ALU.min))
                    link(v.tensor_tensor(eq, src, wide(m), ALU.is_equal))
                    link(v.scalar_tensor_tensor(out=cand.rearrange("p t e -> p (t e)"), in0=eq.rearrange("p t e -> p (t e)"), scalar=-100.0,
                                                in1=eid.rearrange("p t e -> p (t e)"), op0=ALU.mult, op1=ALU.add))
                    link(v.tensor_reduce(id1, cand, AX.X, ALU.min))
                    link(v.tensor_tensor(oh, cand, wide(id1), ALU.is_equal))
                    if m is m1:
                        link(v.scalar_tensor_tensor(out=gt2.rearrange("p t e -> p (t e)"), in0=oh1.rearrange("p t e -> p (t e)"), scalar=2.0,
                                                    in1=gt.rearrange("p t e -> p (t e)"), op0=ALU.mult, op1=ALU.add))
                link(v.tensor_tensor(den, m1, m2, ALU.add))
                link(v.reciprocal(den, den))
                link(v.scalar_tensor_tensor(out=wt1[:, :], in0=m1, scalar=0.5, in1=den, op0=ALU.mult, op1=ALU.mult))
                link(v.scalar_tensor_tensor(out=wt2[:, :], in0=m2, scalar=0.5, in1=den, op0=ALU.mult, op1=ALU.mult))
                link(v.tensor_tensor(msk, oh1, oh2, ALU.add))
                assert done[0] == STAT_MASK, done

            def router_slots():
                oh1, oh2 = rt[:, 4], rt[:, 6]
                slot, tot, inc, tmp = rt[:, 0], rt[:, 1], rt[:, 2], rt[:, 3]
                nt, end, off = (rt[:, 12 + k].rearrange("p t e -> p (t e)")[:, 0:EXPERTS] for k in range(3))
                f1, f2 = (rt[:, 15 + k].rearrange("p t e -> p (t e)")[:, 0:TT] for k in range(2))
                steps128 = csts[:, TT * EXPERTS:TT * EXPERTS + TT]
                tiles = csts[:, TT * EXPERTS + TT:TT * EXPERTS + TT + JT]
                wait_full(dve, "H", ("RP",))
                wait_full(dve, "V", ("RP",))
                v.tensor_copy(tot, bank["V"][:, 0:TT * EXPERTS].rearrange("p (t e) -> p t e", t=TT)).then_inc(free["V"], 1)
                wait_taken(dve, "V", ("RP",))
                dve.wait_ge(ones_set, 1)
                for e in range(EXPERTS):
                    ins = v.tensor_tensor_scan(inc[:, :, e], ones[:, 0:TT], tot[:, :, e], 0.0, ALU.mult, ALU.add)
                link(ins)
                cmp = tmp.rearrange("p t e -> p (t e)").rearrange("p (e k) -> p e k", e=EXPERTS)
                link(v.tensor_tensor(cmp, inc[:, TT - 1, :].unsqueeze(2).to_broadcast([P, EXPERTS, TT]),
                                     steps128.unsqueeze(1).to_broadcast([P, EXPERTS, TT]), ALU.is_gt))
                link(v.tensor_reduce(nt, cmp, AX.X, ALU.add))
                link(v.tensor_tensor_scan(end, ones[:, 0:EXPERTS], nt, 0.0, ALU.mult, ALU.add))
                link(v.tensor_tensor(off, end, nt, ALU.subtract))
                link(v.tensor_tensor(inc, inc, tot, ALU.subtract))
                v.tensor_tensor(slot, inc, bank["H"][:, 0:TT * EXPERTS].rearrange("p (t e) -> p t e", t=TT), ALU.add).then_inc(free["H"], 1)
                wait_taken(dve, "H", ("RP",))
                link(v.tensor_scalar(off, off, float(P), None, ALU.mult))
                link(v.tensor_tensor(slot, slot, off.unsqueeze(1).to_broadcast([P, TT, EXPERTS]), ALU.add))
                for oh, f, sl in ((oh1, f1, sl1), (oh2, f2, sl2)):
                    link(v.tensor_tensor(tmp, oh, slot, ALU.mult))
                    link(v.tensor_reduce(f, tmp, AX.X, ALU.add))
                    link(v.tensor_copy(sl[:, :], f))
                k = JT * EXPERTS
                big = v1[0:1, 20 * TT * EXPERTS:20 * TT * EXPERTS + k].rearrange("p (j e) -> p j e", e=EXPERTS)
                fl = v1[0:1, 24 * TT * EXPERTS:24 * TT * EXPERTS + JT]
                link(v.tensor_tensor(big, tiles[0:1, :].unsqueeze(2).to_broadcast([1, JT, EXPERTS]),
                                     end[0:1, :].unsqueeze(1).to_broadcast([1, JT, EXPERTS]), ALU.is_ge))
                link(v.tensor_reduce(fl, big, AX.X, ALU.add))
                link(v.tensor_scalar(fl, fl, float(EXPERTS - 1), float(WE), ALU.min, ALU.mult))
                link(v.tensor_copy(te[:, :], fl))
                assert done[0] == STAT_END, done

            def do(piece):
                kind = piece[0]
                if kind == "X2":
                    q, c = piece[1], piece[2]
                    dve.wait_ge(tqb, 2 * c + q + 1)
                    if q == 0 and c >= 2:
                        dve.wait_ge(uu, c - 1)
                    v.scalar_tensor_tensor(out=x2[:, c % 2, 2 * q:2 * q + 2, :], in0=tqB[:, :, :], scalar=1.0,
                                           in1=xc[:, 2 * q:2 * q + 2, :], op0=ALU.add, op1=ALU.mult).then_inc(x2r, 1)
                elif kind == "O1":
                    c = piece[2]
                    if c >= 1:
                        wait_full(dve, "V", ("O3", 1, c - 1))
                    dve.wait_ge(dlt, min(c + 2, CHUNKS))
                    for q, b in enumerate("HV"):
                        wait_full(dve, b, piece)
                        for i in range(2):
                            e = 2 * q + i
                            ins = v.scalar_tensor_tensor(out=y1[:, e, :], in0=x2[:, c % 2, e, :], scalar=WD[:, e:e + 1],
                                                         in1=bank[b][:, i * CH:(i + 1) * CH], op0=ALU.mult, op1=ALU.add)
                        ins.then_inc(free[b], 1)
                elif kind == "O2":
                    q, c = piece[1], piece[2]
                    dve.wait_ge(tqo, 2 * c + q + 1)
                    v.scalar_tensor_tensor(out=tqO[:, :, :], in0=tqO[:, :, :], scalar=1.0,
                                           in1=bank["G"][:, :].rearrange("p (k t) -> p k t", k=2),
                                           op0=ALU.add, op1=ALU.mult).then_inc(free["G"], 1)
                elif kind == "RA":
                    router_choice()
                elif kind == "RB":
                    router_slots()
                elif kind == "FA" and piece[1] < JT:
                    j = piece[1]
                    dve.wait_ge(s_th, j + 1)
                    at_least(dve, s_g, j)
                    v.scalar_tensor_tensor(out=g1[:, :], in0=th[:, :], scalar=1.0, in1=bank["H"][:, :],
                                           op0=ALU.add, op1=ALU.mult).then_inc(free["H"], 1)
                elif kind == "S":
                    t = piece[1]
                    i = t % 2
                    dve.wait_ge(ld_s[i], 32 * (t // 2 + 1))
                    v.scalar_tensor_tensor(out=sbuf_m[i], in0=sbuf_x[i], scalar=r1[:, t:t + 1], in1=sbuf_m[i],
                                           op0=ALU.mult, op1=ALU.add).then_inc(sums, 1)
                    dve.wait_ge(gat[i], 32 * (t // 2 + 1))
                    for k, wt in enumerate((wt1, wt2)):
                        dve.wait_ge(sums, 3 * t + k + 1)
                        v.scalar_tensor_tensor(out=sbuf_m[i], in0=gbuf[i][:, k * D:(k + 1) * D], scalar=wt[:, t:t + 1],
                                               in1=sbuf_m[i], op0=ALU.mult, op1=ALU.add).then_inc(sums, 1)

            dve.wait_ge(wprep, 6)
            for piece in prologue():
                do(piece)
            for c in range(CHUNKS):
                at = pieces(c)
                for n in range(N):
                    u = N * c + n
                    scans(u)
                    for piece in at[2 * n]:
                        do(piece)
                    if u >= 1:
                        sum_states(u - 1)
                    for piece in at[2 * n + 1]:
                        do(piece)
            sum_states(N * CHUNKS - 1)
            for piece in epilogue():
                do(piece)


def kernel(L0_attn_resid, L0_attn_norm_w, L0_attn_skip_w, L0_attn_in_w, L0_attn_conv_w, L0_attn_conv_b, L0_attn_wd1,
           L0_attn_wd2, L0_attn_wd2_b, L0_attn_wB, L0_attn_wC, L0_attn_A_log, L0_attn_W_D, L0_attn_out_w,
           L0_ffn_Wr, L0_ffn_W1, L0_ffn_V1, L0_ffn_W2):
    import numpy as np
    import concourse.bacc as bacc
    from concourse.bass_utils import run_bass_kernel_spmd

    a = np.asarray
    column = lambda w: a(w).reshape(-1, P).T
    e_index = np.tile(np.arange(EXPERTS, dtype=np.float32), TT)
    table = np.concatenate([e_index, P * np.arange(TT, dtype=np.float32), np.arange(JT, dtype=np.float32)])
    arrays = {
        "x": a(L0_attn_resid), "norm_w": column(L0_attn_norm_w),
        "skip_wT": a(L0_attn_skip_w).T, "in_wT": a(L0_attn_in_w).T, "conv_w": a(L0_attn_conv_w),
        "conv_b": column(L0_attn_conv_b), "wd1T": a(L0_attn_wd1).T, "wd2T": a(L0_attn_wd2).T, "wd2_b": column(L0_attn_wd2_b),
        "wBCT": np.stack([a(L0_attn_wB).T, a(L0_attn_wC).T]), "A_log": a(L0_attn_A_log), "W_D": column(L0_attn_W_D),
        "out_wT": a(L0_attn_out_w).T, "Wr": a(L0_ffn_Wr), "W1": a(L0_ffn_W1), "V1": a(L0_ffn_V1), "W2": a(L0_ffn_W2),
        "ident": np.eye(P, dtype=np.float32), "tri": np.triu(np.ones((P, P), np.float32), 1),
        "cst": np.tile(table, (P, 1)),
    }
    arrays = {"in_" + k: np.ascontiguousarray(w) for k, w in arrays.items()}
    nc = bacc.Bacc("TRN2", target_bir_lowering=False, num_devices=1, dynamic_dma_scratch_size=8192)
    args = [nc.dram_tensor(k, w.shape, mybir.dt.from_np(w.dtype), kind="ExternalInput").ap() for k, w in arrays.items()]
    out = nc.dram_tensor("out_0", (BATCH, SEQ, D), F32, kind="ExternalOutput").ap()
    mamba_moe(nc, *args, out)
    r = run_bass_kernel_spmd(nc, [arrays], core_ids=[0])
    return r.results[0]["out_0"]
```

```python
import concourse.bass as bass
from concourse import mybir
from contextlib import ExitStack

F32 = mybir.dt.float32
I32 = mybir.dt.int32
ALU = mybir.AluOpType
ACT = mybir.ActivationFunctionType
AX = mybir.AxisListType

P = 128
BATCH, SEQ, D = 4, 1024, 256
E, N, R, TAPS = 512, 16, 128, 4
EXPERTS, FF, TOPK = 8, 512, 2
EPS = 1e-5
TOKENS = BATCH * SEQ
KD, KE = D // P, E // P
CH = 256
SUB = CH // P
CHUNKS = TOKENS // CH
CPB = SEQ // CH
TT = TOKENS // P
JT = TOKENS * TOPK // P + EXPERTS
GROUPS = ((0, SUB), (SUB, TT))
STAT_VAR, STAT_RMS, STAT_LN = (1, 19), (9, 27), (18, 36)
STAT_LOGITS, STAT_MASK, STAT_END = 39, 58, 76
SLOTS = JT * P
WE = KD * FF
assert WE == (FF // P) * D

F_PLACES = [1, 4, 6, 8, 10, 11, 13, 14, 16, 17, 20, 21, 22, 23, 24, 25, 26, 28]
B_PLACES = [(5, ("B1",)), (7, ("B2", 0)), (7, ("CV", 0)), (9, ("B2", 1)), (9, ("CV", 1)), (10, ("X2", 0)),
            (12, ("CV", 2)), (14, ("CV", 3)), (15, ("X2", 1)), (18, ("B3",)), (19, ("B4",)), (20, ("SP",)),
            (21, ("DL",)), (23, ("U",)), (27, ("B5",))]
O_PLACES = [(2, ("O1",)), (3, ("O2", 0)), (5, ("O2", 1)), (12, ("O3", 0)), (15, ("O3", 1))]
LAST_O = 15
R_PLACES = [1, 3, 4, 6, 8, 9, 11, 13, 14, 16, 17, 18, 20, 21, 22, 23, 24, 25]
DVE_CONV = (0, 1, 2, 15)
ACT_PRODUCTS = (1, 14)
RA_PLACES = (26, 28, 29)
RING = 8
FIRST_FFN, LAST_FFN = 2, 14
TPC = JT // (LAST_FFN - FIRST_FFN)
assert TPC * 3 == len(F_PLACES)


def pieces(c):
    at = [[] for _ in range(2 * N)]
    if c >= 1:
        for k, piece in O_PLACES:
            at[k].append(piece + (c - 1,) if len(piece) > 1 else (piece[0], 0, c - 1))
    if c + 1 < CHUNKS:
        for k, piece in B_PLACES:
            at[k].append(piece + (c + 1,) if len(piece) > 1 else (piece[0], 0, c + 1))
    if c == 0:
        for i in range(TT // 2 + 2):
            at[R_PLACES[i]].append(("R", i))
        at[RA_PLACES[0]].append(("RA",))
        at[RA_PLACES[1]].append(("RP",))
        at[RA_PLACES[2]].append(("RB",))
    elif c == 1:
        for i in range(TT // 2):
            at[F_PLACES[i]].append(("D", i))
        at[29].append(("FB", -1))
    elif c < LAST_FFN:
        for k, place in enumerate(F_PLACES):
            at[place].append((("FA", "FB", "FC")[k % 3], TPC * (c - FIRST_FFN) + k // 3))
    elif c == LAST_FFN:
        at[F_PLACES[0]].append(("FA", JT))
        at[F_PLACES[1]].append(("FC", JT))
        for t in range(len(F_PLACES) - 2):
            at[F_PLACES[2 + t]].append(("S", t))
    else:
        first = len(F_PLACES) - 2
        late = [k for k in F_PLACES if k > LAST_O]
        rest = list(range(first, TT - 2))
        for t, k in zip(rest, F_PLACES[:len(rest) - len(late)] + late):
            at[k].append(("S", t))
    return at


def prologue():
    b2 = [("B2", q, 0) for q in range(KE // 2)]
    convs = [("CV", e, 0) for e in range(KE)]
    x2 = [("X2", q, 0) for q in range(KE // 2)]
    return [("B1", 0, 0)] + b2 + convs + x2 + [(k, 0, 0) for k in ("B3", "B4", "SP", "DL", "U")] + [("ST",), ("B5", 0, 0)]


def gpsimd_products(u):
    return 2 * (u + 1) - scalar_products(u)


def scalar_products(u):
    return sum(min(max(u + 1 - N * c, 0), N) for c in ACT_PRODUCTS)


def epilogue():
    return [(p + (CHUNKS - 1,) if len(p) > 1 else (p[0], 0, CHUNKS - 1)) for _, p in O_PLACES] + \
        [("S", TT - 2), ("S", TT - 1)]


def ahead(t):
    if t == 0 or t == TT - SUB:
        return [t, t + 1]
    return [] if t + 1 in (TT - SUB, TT) else [t + 1]


def banks_of(piece):
    kind = piece[0]
    if kind == "B2":
        return ["G"] if piece[1] == 0 else ["V"]
    if kind == "O3":
        return ["H"] if piece[1] == 0 else ["V"]
    if kind == "FA":
        return (["H"] if piece[1] < JT else []) + (["G"] if piece[1] > 0 else [])
    if kind == "FB":
        return (["V"] if piece[1] >= 0 else []) + (["X"] if piece[1] + 1 < JT else [])
    if kind == "FC":
        return ["X"] if piece[1] > 0 else []
    if kind == "R":
        return ["H", "V"] if 1 <= piece[1] <= TT // 2 else []
    return {"B1": ["G"], "B3": ["G"], "B4": ["H", "V"], "B5": ["H", "V"], "O1": ["H", "V"], "O2": ["G"],
            "RP": ["H", "V"]}.get(kind, [])


def count_uses():
    order = list(prologue())
    begins = {}
    uses, count = {}, {"H": 0, "V": 0, "X": 0, "G": 0}

    def walk(piece):
        for b in banks_of(piece):
            uses[b, piece] = count[b]
            count[b] += 1

    for piece in order:
        walk(piece)
    for c in range(CHUNKS):
        begins[c] = dict(count)
        for place in pieces(c):
            for piece in place:
                walk(piece)
    for piece in epilogue():
        walk(piece)
    return uses, begins


def mamba_moe(nc, x, norm_w, skip_wT, in_wT, conv_w, conv_b, wd1T, wd2T, wd2_b, wBCT, A_log, W_D, out_wT,
              Wr, W1, V1, W2, ident, tri, cst, out):
    USES, BEGINS = count_uses()
    ctx = ExitStack()
    with ctx:
        def sb(name, shape, dt=F32):
            return ctx.enter_context(nc.sbuf_tensor(name, shape, dt))

        def sem(name):
            return ctx.enter_context(nc.semaphore(name))

        xbuf = nc.dram_tensor("xbuf", (SLOTS, D), F32, kind="Internal").ap()
        ybuf = nc.dram_tensor("ybuf", (SLOTS, D), F32, kind="Internal").ap()
        mbuf = nc.dram_tensor("mbuf", (TOKENS, D), F32, kind="Internal").ap()
        x_rows = x.rearrange("b l d -> (b l) d")
        out_rows = out.rearrange("b l d -> (b l) d")

        w1 = sb("w1", [P, EXPERTS * WE])
        v1 = sb("v1", [P, EXPERTS * WE])
        w2 = sb("w2", [P, EXPERTS * WE])
        inw = sb("inw", [P, KD, E])
        skw = sb("skw", [P, KD, E])
        wd1 = sb("wd1", [P, KE, R])
        wd2 = sb("wd2", [P, E])
        wbc = sb("wbc", [P, KE, 2 * N])
        outw = sb("outw", [P, KE, D])
        wrt = sb("wrt", [P, KD, EXPERTS])
        cw = sb("cw", [P, KE, TAPS])
        cb = sb("cb", [P, KE])
        db = sb("db", [P, KE])
        Am = sb("Am", [P, KE, N])
        WD = sb("WD", [P, KE])
        nw = sb("nw", [P, KD])
        idn = sb("idn", [P, P])
        edge = sb("edge", [P, KE, TAPS - 1])
        st6 = sb("st6", [P, 2, 6])
        mv = sb("mv", [P, TT, 2])
        sq = sb("sq", [P, TT])
        ta = sb("ta", [P, TT])
        rstd = sb("rstd", [P, TT])
        nmr = sb("nmr", [P, TT])
        s2 = sb("s2", [P, TT])
        nm2 = sb("nm2", [P, TT])
        r1 = sb("r1", [P, TT])
        wt1 = sb("wt1", [P, TT])
        wt2 = sb("wt2", [P, TT])
        sl1 = sb("sl1", [P, TT], I32)
        sl2 = sb("sl2", [P, TT], I32)
        te = sb("te", [1, JT], I32)
        xch = sb("xch", [P, 2, SUB, D])
        rnT = sb("rnT", [P, 2, KD, CH])
        xin = sb("xin", [P, KE, TAPS - 1 + CH])
        xc = sb("xc", [P, KE, CH])
        tap = sb("tap", [P, 2, CH])
        tqB = sb("tqB", [P, 2, CH])
        tqO = sb("tqO", [P, 2, CH])
        x2 = sb("x2", [P, 2, KE, CH])
        delta = sb("delta", [P, 2, KE, CH])
        uT = sb("uT", [P, 2, SUB, E])
        yac = sb("yac", [P, 2, SUB, E])
        y1 = sb("y1", [P, KE, CH])
        BC = sb("BC", [P, 2, SUB, 2 * N])
        dtT = sb("dtT", [P, CH])
        carry = sb("carry", [P, N, KE])
        aexp = sb("aexp", [P, 2, KE, CH])
        ub = sb("ub", [P, 2, SUB, E])
        hb = sb("hb", [P, 2, KE, CH])
        tok = sb("tok", [P, 4, D])
        xT = sb("xT", [P, 2, KD, P])
        th = sb("th", [P, FF])
        g1 = sb("g1", [P, FF])
        vs = sb("vs", [P, FF])
        gT = sb("gT", [P, FF])
        mst = sb("mst", [P, 2, D])
        xall = w1[:, :].rearrange("p (t d) -> p t d", t=TT)
        rt = v1[:, :].rearrange("p (k t e) -> p k t e", k=WE * EXPERTS // (TT * EXPERTS), t=TT)
        trim = w2[:, 0:P]
        ones = w2[:, P:2 * P]
        csts = w2[:, 2 * P:2 * P + cst.shape[1]]

        bps = [ctx.enter_context(nc.psum_tensor(f"bps{i}", [P, 512], F32)) for i in range(2)]
        hps = [ctx.enter_context(nc.psum_tensor(f"hps{i}", [P, 512], F32)) for i in range(2)]
        bank = {b: ctx.enter_context(nc.psum_tensor(f"bank{b}", [P, 512], F32)) for b in "HVXG"}

        ld_first = sem("ld_first")
        ld_small = sem("ld_small")
        ld_late = sem("ld_late")
        ld_x = [sem(f"ld_x{i}") for i in range(4)]
        bst = sem("bst")
        ones_set = sem("ones_set")
        ld_w = sem("ld_w")
        ld_xch = [sem("ld_xch0"), sem("ld_xch1")]
        zero_set = sem("zero_set")
        zeroed = sem("zeroed")
        wprep = sem("wprep")
        aprep = sem("aprep")
        stat = sem("stat")
        sact = sem("sact")
        full = {b: sem("full_" + b) for b in "HVXG"}
        free = {b: sem("free_" + b) for b in "HVXG"}
        z_done = sem("z_done")
        halo = sem("halo")
        conv = sem("conv")
        cvs = sem("cvs")
        cvd = sem("cvd")
        tqb = sem("tqb")
        x2r = sem("x2r")
        dtr = sem("dtr")
        spx = sem("spx")
        dlt = sem("dlt")
        uu = sem("uu")
        tqo = sem("tqo")
        gate = sem("gate")
        m_out = [sem("m_out0"), sem("m_out1")]
        s_ub = sem("s_ub")
        s_uba = sem("s_uba")
        s_bT = sem("s_bT")
        s_a = sem("s_a")
        s_scan = sem("s_scan")
        s_cc = sem("s_cc")
        s_hT = sem("s_hT")
        s_acc = sem("s_acc")
        xn_r = sem("xn_r")
        xTr = sem("xTr")
        lgt = sem("lgt")
        disp = [sem(f"disp{i}") for i in range(RING)]
        ld_xs = [sem("ld_xs0"), sem("ld_xs1")]
        s_th = sem("s_th")
        s_g = sem("s_g")
        y_out = [sem("y_out0"), sem("y_out1")]
        gat = [sem(f"gat{i}") for i in range(2)]
        ld_s = [sem("ld_s0"), sem("ld_s1")]
        sums = sem("sums")
        o_out = [sem("o_out0"), sem("o_out1")]
        block = ctx.enter_context(nc.Block())

        gbuf = [g1[:, :], vs[:, :]]
        sbuf_x = [tok[:, 0, :], tok[:, 1, :]]
        sbuf_m = [tok[:, 2, :], tok[:, 3, :]]

        def at_least(eng, s, value):
            if value > 0:
                eng.wait_ge(s, value)

        def wait_full(eng, b, piece):
            at_least(eng, full[b], USES[b, piece] + 1)

        def wait_free(eng, b, piece):
            at_least(eng, free[b], USES[b, piece])

        def wait_taken(eng, b, piece):
            at_least(eng, free[b], USES[b, piece] + 1)

        FIRST_LOADS, SMALL_LOADS, LATE_LOADS = 5, 7, 5
        ring = [tok[:, k, :] for k in range(4)] + [g1[:, 0:D], g1[:, D:2 * D], vs[:, 0:D], vs[:, D:2 * D]]
        assert len(ring) == RING

        @block.sync
        def _(sp):
            def load_quarter(t):
                sp.dma_start(xall[:, t:t + 8, :], x_rows[t * P:(t + 8) * P, :].rearrange("(t p) d -> p t d", p=P)).then_inc(ld_x[t // 8], 16)

            def load_chunk(c):
                if c >= 2:
                    wait_full(sp, "G", ("B1", 0, c - 2))
                sp.dma_start(xch[:, c % 2, :, :], x_rows[c * CH:(c + 1) * CH, :].rearrange("(s p) d -> p s d", p=P)).then_inc(ld_xch[c % 2], 16)

            def load_tile(j):
                if j >= 2:
                    wait_full(sp, "X", ("FB", j - 3))
                sp.dma_start(tok[:, j % 2, :], xbuf[j * P:(j + 1) * P, :]).then_inc(ld_xs[j % 2], 16)

            def do(piece):
                kind = piece[0]
                if kind == "B1" and piece[2] + 1 < CHUNKS:
                    load_chunk(piece[2] + 1)
                elif kind == "O3":
                    s, c = piece[1], piece[2]
                    wait_taken(sp, "HV"[s], piece)
                    t = SUB * c + s
                    sp.dma_start(mbuf[t * P:(t + 1) * P, :], mst[:, s, :]).then_inc(m_out[s], 16)
                elif kind == "R" and piece[1] < 8:
                    sp.wait_ge(zero_set, 2)
                    a0, a1 = piece[1] * JT // 8, (piece[1] + 1) * JT // 8
                    sp.dma_start(xbuf.rearrange("(p a) d -> p a d", p=P)[:, a0:a1, :],
                                 gT[:, 0:D].unsqueeze(1).to_broadcast([P, a1 - a0, D])).then_inc(zeroed, 16)
                elif kind == "D" and piece[1] == TT // 2 - 1:
                    sp.wait_ge(xn_r, 2 * TT)
                    sp.dma_start(w1[:, :].rearrange("p (e k f) -> p e k f", e=EXPERTS, k=KD), W1.rearrange("e (k p) f -> p e k f", p=P)).then_inc(ld_w, 16)
                elif kind == "RB":
                    sp.wait_ge(stat, STAT_END)
                    sp.dma_start(v1[:, :].rearrange("p (e k f) -> p e k f", e=EXPERTS, k=KD), V1.rearrange("e (k p) f -> p e k f", p=P)).then_inc(ld_w, 16)
                    sp.dma_start(w2[:, :].rearrange("p (e k f) -> p e k f", e=EXPERTS, k=FF // P), W2.rearrange("e (k p) f -> p e k f", p=P)).then_inc(ld_w, 16)
                elif kind == "FB" and piece[1] == -1:
                    for i in range(RING):
                        sp.wait_ge(disp[i], 16 * 2 * TT // RING)
                    load_tile(0)
                    load_tile(1)
                elif kind == "FA" and piece[1] + 2 < JT:
                    load_tile(piece[1] + 2)
                elif kind == "FC" and piece[1] > 0:
                    j = piece[1] - 1
                    wait_taken(sp, "X", piece)
                    sp.dma_start(ybuf[j * P:(j + 1) * P, :], tok[:, 2 + j % 2, :]).then_inc(y_out[j % 2], 16)
                elif kind == "S":
                    t = piece[1]
                    if t == 0:
                        for k in range(2):
                            sp.wait_ge(y_out[k], 16 * JT // 2)
                    for tn in ahead(t):
                        i = tn % 2
                        sp.wait_ge(m_out[i], 16 * (tn // 2 + 1))
                        at_least(sp, o_out[i], 16 * (tn // 2))
                        sp.dma_start(sbuf_x[i], x_rows[tn * P:(tn + 1) * P, :]).then_inc(ld_s[i], 16)
                        sp.dma_start(sbuf_m[i], mbuf[tn * P:(tn + 1) * P, :]).then_inc(ld_s[i], 16)
                    sp.wait_ge(sums, 3 * (t + 1))
                    sp.dma_start(out_rows[t * P:(t + 1) * P, :], sbuf_m[t % 2]).then_inc(o_out[t % 2], 16)

            load_chunk(0)
            sp.dma_start(inw[:, :, :], in_wT.rearrange("(k p) e -> p k e", p=P)).then_inc(ld_first, 16)
            sp.dma_start(wd1[:, :, :], wd1T.rearrange("(k p) r -> p k r", p=P)).then_inc(ld_small, 16)
            sp.dma_start(wd2[:, :], wd2T).then_inc(ld_small, 16)
            for t in range(0, TT, 8):
                load_quarter(t)
            for piece in prologue():
                do(piece)
            for c in range(CHUNKS):
                for place in pieces(c):
                    for piece in place:
                        do(piece)
            for piece in epilogue():
                do(piece)
            for i in range(2):
                sp.wait_ge(o_out[i], 16 * TT // 2)
                sp.wait_ge(m_out[i], 16 * TT // 2)
                sp.wait_ge(y_out[i], 16 * JT // 2)

        @block.scalar
        def _(act):
            for done, loads in (
                (ld_first, [(idn[:, :], ident), (nw[:, :], norm_w),
                            (cw[:, :, :], conv_w.rearrange("(k p) w -> p k w", p=P)), (cb[:, :], conv_b)]),
                (ld_small, [(Am[:, :, :], A_log.rearrange("(k p) n -> p k n", p=P)),
                            (wbc[:, :, 0:N], wBCT[0].rearrange("(k p) n -> p k n", p=P)),
                            (wbc[:, :, N:2 * N], wBCT[1].rearrange("(k p) n -> p k n", p=P)),
                            (db[:, :], wd2_b), (WD[:, :], W_D)]),
                (ld_late, [(outw[:, :, :], out_wT.rearrange("(k p) d -> p k d", p=P)),
                           (wrt[:, :, :], Wr.rearrange("(k p) e -> p k e", p=P)),
                           (skw[:, :, :], skip_wT.rearrange("(k p) e -> p k e", p=P)),
                           (trim, tri), (csts, cst)]),
            ):
                for dst, src in loads:
                    act.dma_start(dst, src).then_inc(done, 16)

            def roots(g):
                t0, t1 = GROUPS[g]
                for step in (STAT_VAR, STAT_RMS):
                    act.wait_ge(stat, step[g])
                    nc.scalar.activation(sq[:, t0:t1], ta[:, t0:t1], ACT.Sqrt).then_inc(sact, 1)
                act.wait_ge(stat, STAT_LN[g])

            roots(0)
            act.wait_ge(ld_first, 16 * FIRST_LOADS)

            def exps(u):
                c, n = divmod(u, N)
                if n == 0:
                    act.wait_ge(dlt, c + 1)
                for e in range(KE):
                    at_least(act, s_scan, 4 * (u - 2) + e + 1)
                    nc.scalar.activation(aexp[:, u % 2, e, :], delta[:, c % 2, e, :], ACT.Exp,
                                         scale=Am[:, e, n:n + 1]).then_inc(s_a, 1)
                if c in ACT_PRODUCTS:
                    wait_taken(act, "V", ("B5", 0, c))
                    act.wait_ge(s_bT, 2 * (u - 1))
                    nc.scalar.activation(ub[:, u % 2, 1, :], uT[:, c % 2, 1, :], ACT.Identity,
                                         scale=BC[:, c % 2, 1, n:n + 1]).then_inc(s_uba, 1)

            def do(piece):
                kind = piece[0]
                if kind == "B1":
                    c = piece[2]
                    act.wait_ge(ld_xch[c % 2], 16 * (c // 2 + 1))
                    for s in range(SUB):
                        t = SUB * c + s
                        nc.scalar.activation(xch[:, c % 2, s, :], xch[:, c % 2, s, :], ACT.Identity,
                                             bias=nm2[:, t:t + 1], scale=s2[:, t:t + 1]).then_inc(z_done, 1)
                    wait_full(act, "G", piece)
                    if c >= 2:
                        wait_full(act, "G", ("O2", 1, c - 2))
                    for k in range(KD):
                        ins = nc.scalar.activation(rnT[:, c % 2, k, :], bank["G"][:, k * CH:(k + 1) * CH], ACT.Identity,
                                                   scale=nw[:, k:k + 1])
                    ins.then_inc(free["G"], 1)
                elif kind == "B2":
                    q, c = piece[1], piece[2]
                    b = "G" if q == 0 else "V"
                    at_least(act, conv, KE * c)
                    if q == 0:
                        if c % CPB == 0:
                            if c == 0:
                                act.wait_ge(zero_set, 2)
                            src = edge[:, :, :]
                        else:
                            src = xin[:, :, CH:CH + TAPS - 1]
                        nc.scalar.activation(xin[:, :, 0:TAPS - 1], src, ACT.Copy).then_inc(halo, 1)
                    act.wait_ge(halo, c + 1)
                    wait_full(act, b, piece)
                    nc.scalar.activation(xin[:, 2 * q:2 * q + 2, TAPS - 1:], bank[b][:, :].rearrange("p (k t) -> p k t", k=2),
                                         ACT.Copy).then_inc(free[b], 1)
                elif kind == "X2":
                    q, c = piece[1], piece[2]
                    act.wait_ge(conv, KE * c + 2 * q + 2)
                    at_least(act, x2r, 2 * c + q)
                    nc.scalar.activation(tqB[:, :, :], xc[:, 2 * q:2 * q + 2, :], ACT.Tanh, scale=0.5).then_inc(tqb, 1)
                elif kind == "B3":
                    c = piece[2]
                    wait_full(act, "G", piece)
                    at_least(act, s_ub, gpsimd_products(N * (c - 1) - 1))
                    at_least(act, s_uba, scalar_products(N * (c - 1) - 1))
                    at_least(act, s_acc, 2 * N * (c - 1))
                    if c >= 1:
                        wait_full(act, "V", ("B4", 0, c - 1))
                    nc.scalar.activation(dtT[:, :], bank["G"][:, 0:CH], ACT.Copy)
                    nc.scalar.activation(BC[:, c % 2, :, :], bank["G"][:, CH:CH + SUB * 2 * N].rearrange("p (s n) -> p s n", s=SUB),
                                         ACT.Copy).then_inc(free["G"], 1)
                elif kind == "B4":
                    c = piece[2]
                    if c >= 1:
                        at_least(act, dlt, c)
                    if c >= 2:
                        wait_full(act, "V", ("O3", 1, c - 2))
                        act.wait_ge(uu, c - 1)
                    for q, b in enumerate("HV"):
                        wait_full(act, b, piece)
                        for i in range(2):
                            e = 2 * q + i
                            nc.scalar.activation(y1[:, e, :], bank[b][:, i * CH:(i + 1) * CH], ACT.Abs,
                                                 bias=db[:, e:e + 1]).then_inc(spx, 1)
                            ins = nc.scalar.activation(delta[:, c % 2, e, :], bank[b][:, i * CH:(i + 1) * CH], ACT.Relu,
                                                       bias=db[:, e:e + 1])
                        ins.then_inc(free[b], 1)
                elif kind == "SP":
                    c = piece[2]
                    act.wait_ge(spx, 6 * c + 4)
                    nc.scalar.activation(y1[:, :, :], y1[:, :, :], ACT.Exp, scale=-1.0).then_inc(spx, 1)
                    act.wait_ge(spx, 6 * c + 5)
                    nc.scalar.activation(y1[:, :, :], y1[:, :, :], ACT.Ln, bias=1.0).then_inc(spx, 1)
                elif kind == "B5":
                    c = piece[2]
                    at_least(act, s_ub, gpsimd_products(N * (c - 1) - 1))
                    at_least(act, s_uba, scalar_products(N * (c - 1) - 1))
                    for s, b in enumerate("HV"):
                        wait_full(act, b, piece)
                        nc.scalar.activation(uT[:, c % 2, s, :], bank[b][:, :], ACT.Copy).then_inc(free[b], 1)
                elif kind == "O2":
                    q, c = piece[1], piece[2]
                    wait_full(act, "G", piece)
                    at_least(act, gate, 2 * c + q)
                    nc.scalar.activation(tqO[:, :, :], bank["G"][:, :].rearrange("p (k t) -> p k t", k=2), ACT.Tanh,
                                         scale=0.5).then_inc(tqo, 1)
                elif kind == "O3":
                    s, c = piece[1], piece[2]
                    b = "HV"[s]
                    t = SUB * c + s
                    wait_full(act, b, piece)
                    at_least(act, m_out[s], 16 * c)
                    nc.scalar.activation(mst[:, s, :], bank[b][:, 0:D], ACT.Identity, bias=nmr[:, t:t + 1]).then_inc(free[b], 1)
                elif kind == "R":
                    i = piece[1]
                    if i < TT // 2:
                        if i >= 2:
                            wait_full(act, "V", ("R", i - 1))
                        for t in (2 * i, 2 * i + 1):
                            nc.scalar.activation(tok[:, t % 4, :], xall[:, t, :], ACT.Identity, bias=nmr[:, t:t + 1],
                                                 scale=rstd[:, t:t + 1]).then_inc(xn_r, 1)
                    if 1 <= i <= TT // 2:
                        for k, t in enumerate((2 * i - 2, 2 * i - 1)):
                            wait_full(act, "HV"[k], piece)
                            at_least(act, lgt, t - 1)
                            nc.scalar.activation(xT[:, k, :, :], bank["HV"[k]][:, 0:D].rearrange("p (k t) -> p k t", k=KD),
                                                 ACT.Copy).then_inc(free["HV"[k]], 1)
                elif kind == "RA":
                    act.wait_ge(stat, STAT_LOGITS)
                    nc.scalar.activation(rt[:, 1], rt[:, 0], ACT.Exp).then_inc(sact, 1)
                elif kind == "D":
                    for t in (2 * piece[1], 2 * piece[1] + 1):
                        if t < RING:
                            wait_full(act, "V", ("R", TT // 2))
                        else:
                            act.wait_ge(disp[t % RING], 16 * 2 * (t // RING))
                        nc.scalar.activation(ring[t % RING], xall[:, t, :], ACT.Identity, bias=nmr[:, t:t + 1],
                                             scale=rstd[:, t:t + 1]).then_inc(xn_r, 1)
                elif kind == "FA":
                    j = piece[1]
                    if j < JT:
                        wait_full(act, "H", piece)
                        nc.scalar.activation(th[:, :], bank["H"][:, :], ACT.Tanh, scale=0.5).then_inc(s_th, 1)
                    if j > 0:
                        wait_full(act, "G", piece)
                        if j > 1:
                            wait_full(act, "X", ("FC", j - 1))
                        nc.scalar.activation(gT[:, :], bank["G"][:, :], ACT.Copy).then_inc(free["G"], 1)
                elif kind == "FB":
                    j = piece[1]
                    if j + 1 < JT:
                        wait_full(act, "X", piece)
                        if j < 0:
                            act.wait_ge(lgt, TT)
                        nc.scalar.activation(xT[:, (j + 1) % 2, :, :], bank["X"][:, 0:D].rearrange("p (k t) -> p k t", k=KD),
                                             ACT.Copy).then_inc(free["X"], 1)
                    if j >= 0:
                        wait_full(act, "V", piece)
                        nc.scalar.activation(vs[:, :], bank["V"][:, :], ACT.Copy).then_inc(free["V"], 1)
                elif kind == "FC" and piece[1] > 0:
                    j = piece[1] - 1
                    wait_full(act, "X", piece)
                    if j < 2:
                        act.wait_ge(disp[2 + j % 2], 16 * 2 * TT // RING)
                    else:
                        act.wait_ge(y_out[j % 2], 16 * (j // 2))
                    nc.scalar.activation(tok[:, 2 + j % 2, :], bank["X"][:, 0:D], ACT.Copy).then_inc(free["X"], 1)

            for piece in prologue():
                if piece == ("X2", 0, 0):
                    act.wait_ge(ld_small, 16 * SMALL_LOADS)
                    nc.scalar.activation(Am[:, :, :], Am[:, :, :], ACT.Exp).then_inc(aprep, 1)
                if piece == ("ST",):
                    roots(1)
                do(piece)
            act.wait_ge(wprep, 5)
            exps(0)
            for c in range(CHUNKS):
                at = pieces(c)
                for n in range(N):
                    if N * c + n + 1 < N * CHUNKS:
                        exps(N * c + n + 1)
                    for piece in at[2 * n] + at[2 * n + 1]:
                        do(piece)
            for piece in epilogue():
                do(piece)

        @block.gpsimd
        def _(pool):
            nc.gpsimd.memset(gT[:, :], 0.0).then_inc(zero_set, 1)
            nc.gpsimd.memset(edge[:, :, :], 0.0).then_inc(zero_set, 1)
            pool.wait_ge(ld_small, 16 * SMALL_LOADS)
            for w, k in ((wd1[:, :, :], 0.5), (wbc[:, :, 0:N], 0.25), (wbc[:, :, N:2 * N], 0.5), (WD[:, :], 0.5)):
                nc.gpsimd.tensor_scalar(w, w, k, 1.0, ALU.mult, ALU.mult).then_inc(wprep, 1)
            pool.wait_ge(aprep, 1)
            nc.gpsimd.tensor_scalar(Am[:, :, :], Am[:, :, :], -1.0, 1.0, ALU.mult, ALU.mult).then_inc(wprep, 1)
            pool.wait_ge(ld_late, 16 * LATE_LOADS)
            nc.gpsimd.tensor_scalar(outw[:, :, :], outw[:, :, :], 0.5, 1.0, ALU.mult, ALU.mult).then_inc(wprep, 1)

            def products(u):
                c, n = divmod(u, N)
                if n == 0:
                    wait_taken(pool, "V", ("B5", 0, c))
                at_least(pool, s_bT, 2 * (u - 1))
                for s in range(1 if c in ACT_PRODUCTS else SUB):
                    nc.gpsimd.tensor_scalar(ub[:, u % 2, s, :], uT[:, c % 2, s, :], BC[:, c % 2, s, n:n + 1], 1.0,
                                            ALU.mult, ALU.mult).then_inc(s_ub, 1)

            def do(piece):
                kind = piece[0]
                if kind == "CV" and piece[2] not in DVE_CONV:
                    e, c = piece[1], piece[2]
                    b = "G" if e < 2 else "V"
                    wait_taken(pool, b, ("B2", e // 2, c))
                    if c >= 1:
                        wait_full(pool, "V", ("B5", 0, c - 1))
                    first = 6 * (KE * (c - len([k for k in DVE_CONV if k < c])) + e)

                    def product(dst, w, add):
                        return nc.gpsimd.tensor_scalar(dst, xin[:, e, w:w + CH], cw[:, e, w:w + 1], add,
                                                       ALU.mult, ALU.mult if w else ALU.add)

                    product(xc[:, e, :], 0, cb[:, e:e + 1]).then_inc(cvs, 1)
                    product(tap[:, 0, :], 1, 1.0).then_inc(cvs, 1)
                    product(tap[:, 1, :], 2, 1.0).then_inc(cvs, 1)
                    pool.wait_ge(cvs, first + 3)
                    nc.gpsimd.tensor_tensor(xc[:, e, :], xc[:, e, :], tap[:, 0, :], ALU.add).then_inc(cvs, 1)
                    pool.wait_ge(cvs, first + 4)
                    product(tap[:, 0, :], 3, 1.0).then_inc(cvs, 1)
                    nc.gpsimd.tensor_tensor(xc[:, e, :], xc[:, e, :], tap[:, 1, :], ALU.add).then_inc(cvs, 1)
                    pool.wait_ge(cvs, first + 6)
                    nc.gpsimd.tensor_tensor(xc[:, e, :], xc[:, e, :], tap[:, 0, :], ALU.add).then_inc(conv, 1)
                    pool.wait_ge(conv, KE * c + e + 1)
                elif kind == "DL":
                    c = piece[2]
                    pool.wait_ge(spx, 6 * c + 6)
                    wait_taken(pool, "V", ("B4", 0, c))
                    nc.gpsimd.tensor_tensor(delta[:, c % 2, :, :], delta[:, c % 2, :, :], y1[:, :, :], ALU.add).then_inc(dlt, 1)
                elif kind == "U":
                    c = piece[2]
                    pool.wait_ge(dlt, c + 1)
                    pool.wait_ge(x2r, 2 * c + 2)
                    nc.gpsimd.tensor_tensor(xc[:, :, :], delta[:, c % 2, :, :], x2[:, c % 2, :, :], ALU.mult).then_inc(uu, 1)
                elif kind == "O2":
                    q, c = piece[1], piece[2]
                    wait_taken(pool, "G", piece)
                    wait_taken(pool, "HV"[q], ("O1", 0, c))
                    nc.gpsimd.tensor_tensor(y1[:, 2 * q:2 * q + 2, :], y1[:, 2 * q:2 * q + 2, :], tqO[:, :, :],
                                            ALU.mult).then_inc(gate, 1)
                elif kind == "D":
                    if piece[1] == 0:
                        pool.wait_ge(zeroed, 16 * 8)
                        pool.wait_ge(stat, STAT_END)
                    for t in (2 * piece[1], 2 * piece[1] + 1):
                        pool.wait_ge(xn_r, TT + t + 1)
                        for sl in (sl1, sl2):
                            nc.gpsimd.indirect_dma_start(
                                out=xbuf, out_offset=bass.IndirectOffsetOnAxis(ap=sl[:, t:t + 1], axis=0),
                                in_=ring[t % RING], in_offset=None).then_inc(disp[t % RING], 16)
                elif kind == "FB" and piece[1] >= 0:
                    j = piece[1]
                    wait_taken(pool, "V", piece)
                    wait_taken(pool, "H", ("FA", j))
                    nc.gpsimd.tensor_tensor(vs[:, :], g1[:, :], vs[:, :], ALU.mult).then_inc(s_g, 1)
                elif kind == "S":
                    t = piece[1]
                    if t == 0:
                        for k in range(2):
                            pool.wait_ge(y_out[k], 16 * JT // 2)
                    for tn in ahead(t):
                        at_least(pool, sums, 3 * (tn - 1))
                        for k, sl in enumerate((sl1, sl2)):
                            nc.gpsimd.indirect_dma_start(
                                out=gbuf[tn % 2][:, k * D:(k + 1) * D], out_offset=None, in_=ybuf,
                                in_offset=bass.IndirectOffsetOnAxis(ap=sl[:, tn:tn + 1], axis=0)).then_inc(gat[tn % 2], 16)

            for piece in prologue():
                do(piece)
            products(0)
            for c in range(CHUNKS):
                at = pieces(c)
                for n in range(N):
                    u = N * c + n
                    if u + 1 < N * CHUNKS:
                        products(u + 1)
                    for piece in at[2 * n]:
                        do(piece)
                    pool.wait_ge(s_scan, 4 * u + 4)
                    nc.gpsimd.tensor_copy(carry[:, n, :], hb[:, u % 2, :, CH - 1]).then_inc(s_cc, 1)
                    for piece in at[2 * n + 1]:
                        do(piece)
            for piece in epilogue():
                do(piece)

        @block.tensor
        def _(pe):
            pe.wait_ge(ld_first, 16 * FIRST_LOADS)

            def turn_products(u):
                pe.wait_ge(s_ub, gpsimd_products(u))
                at_least(pe, s_uba, scalar_products(u))
                for q in range(2):
                    at_least(pe, s_scan, 4 * (u - 1) + 2 * q + 2)
                    for s in range(SUB):
                        for i in range(2):
                            e = 2 * q + i
                            mm = pe.transpose(bps[q][:, i * CH + s * P:i * CH + (s + 1) * P],
                                              ub[:, u % 2, s, e * P:(e + 1) * P], idn[:, :])
                    mm.then_inc(s_bT, 1)

            def turn_states(u):
                pe.wait_ge(s_scan, 4 * u + 4)
                for s in range(SUB):
                    at_least(pe, s_acc, 2 * (u - 1) + s + 1)
                    for e in range(KE):
                        mm = pe.transpose(hps[s][:, e * P:(e + 1) * P], hb[:, u % 2, e, s * P:(s + 1) * P], idn[:, :])
                    mm.then_inc(s_hT, 1)

            def do(piece):
                kind = piece[0]
                if kind == "B1":
                    c = piece[2]
                    wait_free(pe, "G", piece)
                    for s in range(SUB):
                        pe.wait_ge(z_done, SUB * c + s + 1)
                        for k in range(KD):
                            mm = pe.transpose(bank["G"][:, k * CH + s * P:k * CH + (s + 1) * P],
                                              xch[:, c % 2, s, k * P:(k + 1) * P], idn[:, :])
                    mm.then_inc(full["G"], 1)
                elif kind == "B2" or kind == "O2":
                    q, c = piece[1], piece[2]
                    b = "G" if q == 0 or kind == "O2" else "V"
                    w = inw if kind == "B2" else skw
                    wait_free(pe, b, piece)
                    wait_taken(pe, "G", ("B1", 0, c))
                    for i in range(2):
                        e = 2 * q + i
                        for k in range(KD):
                            mm = pe.matmul(bank[b][:, i * CH:(i + 1) * CH], w[:, k, e * P:(e + 1) * P],
                                           rnT[:, c % 2, k, :], start=(k == 0), stop=(k == KD - 1))
                    mm.then_inc(full[b], 1)
                elif kind == "B3":
                    c = piece[2]
                    wait_free(pe, "G", piece)
                    pe.wait_ge(x2r, 2 * c + 2)
                    if c == 0:
                        pe.wait_ge(wprep, 5)
                    for k in range(KE):
                        pe.matmul(bank["G"][:, 0:CH], wd1[:, k, :], x2[:, c % 2, k, :], start=(k == 0), stop=(k == KE - 1))
                    for s in range(SUB):
                        for k in range(KE):
                            mm = pe.matmul(bank["G"][:, CH + s * 2 * N:CH + (s + 1) * 2 * N], x2[:, c % 2, k, s * P:(s + 1) * P],
                                           wbc[:, k, :], start=(k == 0), stop=(k == KE - 1))
                    mm.then_inc(full["G"], 1)
                elif kind == "B4":
                    c = piece[2]
                    wait_taken(pe, "G", ("B3", 0, c))
                    for q, b in enumerate("HV"):
                        wait_free(pe, b, piece)
                        for i in range(2):
                            e = 2 * q + i
                            mm = pe.matmul(bank[b][:, i * CH:(i + 1) * CH], wd2[:, e * P:(e + 1) * P], dtT[:, :],
                                           start=True, stop=True)
                        mm.then_inc(full[b], 1)
                elif kind == "B5":
                    c = piece[2]
                    pe.wait_ge(uu, c + 1)
                    for s, b in enumerate("HV"):
                        wait_free(pe, b, piece)
                        for e in range(KE):
                            mm = pe.transpose(bank[b][:, e * P:(e + 1) * P], xc[:, e, s * P:(s + 1) * P], idn[:, :])
                        mm.then_inc(full[b], 1)
                elif kind == "O1":
                    c = piece[2]
                    pe.wait_ge(s_acc, 2 * N * (c + 1))
                    for q, b in enumerate("HV"):
                        wait_free(pe, b, piece)
                        for s in range(SUB):
                            for i in range(2):
                                e = 2 * q + i
                                mm = pe.transpose(bank[b][:, i * CH + s * P:i * CH + (s + 1) * P],
                                                  yac[:, c % 2, s, e * P:(e + 1) * P], idn[:, :])
                        mm.then_inc(full[b], 1)
                elif kind == "O3":
                    s, c = piece[1], piece[2]
                    b = "HV"[s]
                    wait_free(pe, b, piece)
                    pe.wait_ge(gate, 2 * c + 2)
                    for k in range(KE):
                        mm = pe.matmul(bank[b][:, 0:D], y1[:, k, s * P:(s + 1) * P], outw[:, k, :],
                                       start=(k == 0), stop=(k == KE - 1))
                    mm.then_inc(full[b], 1)
                elif kind == "R":
                    i = piece[1]
                    if i == 0:
                        pe.wait_ge(wprep, 6)
                    if i >= 2:
                        for k, t in enumerate((2 * i - 4, 2 * i - 3)):
                            wait_taken(pe, "HV"[k], ("R", i - 1))
                            for kd in range(KD):
                                mm = pe.matmul(bank["X"][:, t * EXPERTS:(t + 1) * EXPERTS], xT[:, k, kd, :], wrt[:, kd, :],
                                               start=(kd == 0), stop=(kd == KD - 1))
                            mm.then_inc(lgt, 1)
                    if 1 <= i <= TT // 2:
                        for k, t in enumerate((2 * i - 2, 2 * i - 1)):
                            wait_free(pe, "HV"[k], piece)
                            pe.wait_ge(xn_r, t + 1)
                            for kd in range(KD):
                                mm = pe.transpose(bank["HV"[k]][:, kd * P:(kd + 1) * P], tok[:, t % 4, kd * P:(kd + 1) * P], idn[:, :])
                            mm.then_inc(full["HV"[k]], 1)
                elif kind == "RP":
                    pe.wait_ge(stat, STAT_MASK)
                    pe.wait_ge(ones_set, 1)
                    for b, w in (("H", trim), ("V", ones)):
                        wait_free(pe, b, piece)
                        pe.matmul(bank[b][:, 0:TT * EXPERTS], w, rt[:, 7].rearrange("p t e -> p (t e)"), start=True, stop=True).then_inc(full[b], 1)
                elif kind == "FA":
                    j = piece[1]
                    if j < JT:
                        if j == 0:
                            pe.wait_ge(ld_w, 48)
                        col = pe.value_load(te[0:1, j:j + 1], min_val=0, max_val=(EXPERTS - 1) * WE)
                        columns[j] = col
                        wait_taken(pe, "X", ("FB", j - 1))
                        wait_free(pe, "H", piece)
                        for k in range(KD):
                            mm = pe.matmul(bank["H"][:, :], xT[:, j % 2, k, :], w1[:, bass.ds(col + k * FF, FF)],
                                           start=(k == 0), stop=(k == KD - 1))
                        mm.then_inc(full["H"], 1)
                    if j > 0:
                        wait_free(pe, "G", piece)
                        pe.wait_ge(s_g, j)
                        for k in range(FF // P):
                            mm = pe.transpose(bank["G"][:, k * P:(k + 1) * P], vs[:, k * P:(k + 1) * P], idn[:, :])
                        mm.then_inc(full["G"], 1)
                elif kind == "FB":
                    j = piece[1]
                    if j + 1 < JT:
                        if j < 0:
                            pe.wait_ge(lgt, TT)
                        pe.wait_ge(ld_xs[(j + 1) % 2], 16 * ((j + 1) // 2 + 1))
                        wait_free(pe, "X", piece)
                        for k in range(KD):
                            mm = pe.transpose(bank["X"][:, k * P:(k + 1) * P], tok[:, (j + 1) % 2, k * P:(k + 1) * P], idn[:, :])
                        mm.then_inc(full["X"], 1)
                    if j >= 0:
                        wait_free(pe, "V", piece)
                        for k in range(KD):
                            mm = pe.matmul(bank["V"][:, :], xT[:, j % 2, k, :], v1[:, bass.ds(columns[j] + k * FF, FF)],
                                           start=(k == 0), stop=(k == KD - 1))
                        mm.then_inc(full["V"], 1)
                elif kind == "FC" and piece[1] > 0:
                    j = piece[1] - 1
                    wait_taken(pe, "G", ("FA", j + 1))
                    wait_free(pe, "X", piece)
                    for k in range(FF // P):
                        mm = pe.matmul(bank["X"][:, 0:D], gT[:, k * P:(k + 1) * P], w2[:, bass.ds(columns[j] + k * D, D)],
                                       start=(k == 0), stop=(k == FF // P - 1))
                    mm.then_inc(full["X"], 1)

            columns = {}
            for piece in prologue():
                do(piece)
            for c in range(CHUNKS):
                at = pieces(c)
                for n in range(N):
                    u = N * c + n
                    turn_products(u)
                    for piece in at[2 * n]:
                        do(piece)
                    if u >= 1:
                        turn_states(u - 1)
                    for piece in at[2 * n + 1]:
                        do(piece)
            turn_states(N * CHUNKS - 1)
            for piece in epilogue():
                do(piece)

        @block.vector
        def _(dve):
            done = [0]

            def link(ins):
                done[0] += 1
                ins.then_inc(stat, 1)
                dve.wait_ge(stat, done[0])

            v = nc.vector
            v.memset(ones, 1.0).then_inc(ones_set, 1)
            def statistics(g):
                t0, t1 = GROUPS[g]
                for t in range(t0, t1):
                    if g == 0:
                        dve.wait_ge(ld_xch[0], 16)
                    elif t == t0 or t % 8 == 0:
                        dve.wait_ge(ld_x[t // 8], 16)
                    at_least(dve, bst, 2 * t - 2)
                    v.bn_stats(st6[:, t % 2, :], xch[:, 0, t, :] if g == 0 else xall[:, t, :]).then_inc(bst, 1)
                    dve.wait_ge(bst, 2 * t + 1)
                    v.bn_aggr(mv[:, t, :], st6[:, t % 2, :]).then_inc(bst, 1)
                dve.wait_ge(bst, 2 * t1)
                mean, var = mv[:, t0:t1, 0], mv[:, t0:t1, 1]
                root, under, rs, s, r = (a[:, t0:t1] for a in (sq, ta, rstd, s2, r1))

                def inverse_root(dst):
                    link(v.reciprocal(dst, root))
                    link(v.tensor_tensor(root, dst, dst, ALU.mult))
                    link(v.tensor_tensor(root, root, under, ALU.mult))
                    link(v.tensor_scalar(root, root, -0.5, 1.5, ALU.mult, ALU.add))
                    link(v.tensor_tensor(dst, dst, root, ALU.mult))

                link(v.tensor_scalar(under, var, EPS, None, ALU.add))
                dve.wait_ge(sact, 2 * g + 1)
                inverse_root(rs)
                link(v.tensor_tensor(r, rs, rs, ALU.mult))
                link(v.tensor_tensor(r, r, var, ALU.mult))
                link(v.tensor_scalar(under, r, EPS, None, ALU.add))
                assert done[0] == STAT_RMS[g]
                dve.wait_ge(sact, 2 * g + 2)
                inverse_root(s)
                link(v.tensor_tensor(s, s, rs, ALU.mult))
                link(v.scalar_tensor_tensor(out=nmr[:, t0:t1], in0=mean, scalar=-1.0, in1=rs, op0=ALU.mult, op1=ALU.mult))
                link(v.scalar_tensor_tensor(out=nm2[:, t0:t1], in0=mean, scalar=-1.0, in1=s, op0=ALU.mult, op1=ALU.mult))
                link(v.tensor_scalar(r, rs, 1.0, None, ALU.add))
                assert done[0] == STAT_LN[g]

            statistics(0)

            def scans(u):
                c, n = divmod(u, N)
                at_least(dve, s_hT, 2 * (u - 1))
                at_least(dve, s_cc, u - 1)
                for e in range(KE):
                    dve.wait_ge(s_a, 4 * u + e + 1)
                    if e % 2 == 0:
                        dve.wait_ge(s_bT, 2 * u + e // 2 + 1)
                    first = 0.0 if c % CPB == 0 else carry[:, n, e:e + 1]
                    v.tensor_tensor_scan(hb[:, u % 2, e, :], aexp[:, u % 2, e, :], bps[e // 2][:, (e % 2) * CH:(e % 2 + 1) * CH],
                                         first, ALU.mult, ALU.add).then_inc(s_scan, 1)

            def sum_states(u):
                c, n = divmod(u, N)
                if n == 0 and c >= 2:
                    wait_full(dve, "V", ("O1", 0, c - 2))
                for s in range(SUB):
                    dve.wait_ge(s_hT, 2 * u + s + 1)
                    at_least(dve, s_acc, 2 * (u - 1) + s + 1)
                    scale = BC[:, c % 2, s, N + n:N + n + 1]
                    if n == 0:
                        ins = v.tensor_scalar(yac[:, c % 2, s, :], hps[s][:, :], scale, None, ALU.mult)
                    else:
                        ins = v.scalar_tensor_tensor(out=yac[:, c % 2, s, :], in0=hps[s][:, :], scalar=scale,
                                                     in1=yac[:, c % 2, s, :], op0=ALU.mult, op1=ALU.add)
                    ins.then_inc(s_acc, 1)

            def router_choice():
                lg, gt, eq, cand, oh1, gt2, oh2, msk = (rt[:, k] for k in range(8))
                small = [rt[:, 8 + k].rearrange("p t e -> p (t e)")[:, 0:TT] for k in range(4)]
                m1, m2, id1, den = small
                wide = lambda a: a.unsqueeze(2).to_broadcast([P, TT, EXPERTS])
                eid = csts[:, 0:TT * EXPERTS].rearrange("p (t e) -> p t e", t=TT)
                dve.wait_ge(lgt, TT)
                link(v.tensor_copy(lg, bank["X"][:, 0:TT * EXPERTS].rearrange("p (t e) -> p t e", t=TT)))
                link(v.tensor_reduce(m1, lg, AX.X, ALU.max))
                link(v.tensor_tensor(lg, lg, wide(m1), ALU.subtract))
                assert done[0] == STAT_LOGITS, done
                dve.wait_ge(sact, 5)
                link(v.tensor_reduce(den, gt, AX.X, ALU.add))
                link(v.reciprocal(den, den))
                link(v.tensor_tensor(gt, gt, wide(den), ALU.mult))
                for src, m, oh in ((gt, m1, oh1), (gt2, m2, oh2)):
                    link(v.tensor_reduce(m, src, AX.X, ALU.min))
                    link(v.tensor_tensor(eq, src, wide(m), ALU.is_equal))
                    link(v.scalar_tensor_tensor(out=cand.rearrange("p t e -> p (t e)"), in0=eq.rearrange("p t e -> p (t e)"), scalar=-100.0,
                                                in1=eid.rearrange("p t e -> p (t e)"), op0=ALU.mult, op1=ALU.add))
                    link(v.tensor_reduce(id1, cand, AX.X, ALU.min))
                    link(v.tensor_tensor(oh, cand, wide(id1), ALU.is_equal))
                    if m is m1:
                        link(v.scalar_tensor_tensor(out=gt2.rearrange("p t e -> p (t e)"), in0=oh1.rearrange("p t e -> p (t e)"), scalar=2.0,
                                                    in1=gt.rearrange("p t e -> p (t e)"), op0=ALU.mult, op1=ALU.add))
                link(v.tensor_tensor(den, m1, m2, ALU.add))
                link(v.reciprocal(den, den))
                link(v.scalar_tensor_tensor(out=wt1[:, :], in0=m1, scalar=0.5, in1=den, op0=ALU.mult, op1=ALU.mult))
                link(v.scalar_tensor_tensor(out=wt2[:, :], in0=m2, scalar=0.5, in1=den, op0=ALU.mult, op1=ALU.mult))
                link(v.tensor_tensor(msk, oh1, oh2, ALU.add))
                assert done[0] == STAT_MASK, done

            def router_slots():
                oh1, oh2 = rt[:, 4], rt[:, 6]
                slot, tot, inc, tmp = rt[:, 0], rt[:, 1], rt[:, 2], rt[:, 3]
                nt, end, off = (rt[:, 12 + k].rearrange("p t e -> p (t e)")[:, 0:EXPERTS] for k in range(3))
                f1, f2 = (rt[:, 15 + k].rearrange("p t e -> p (t e)")[:, 0:TT] for k in range(2))
                steps128 = csts[:, TT * EXPERTS:TT * EXPERTS + TT]
                tiles = csts[:, TT * EXPERTS + TT:TT * EXPERTS + TT + JT]
                wait_full(dve, "H", ("RP",))
                wait_full(dve, "V", ("RP",))
                v.tensor_copy(tot, bank["V"][:, 0:TT * EXPERTS].rearrange("p (t e) -> p t e", t=TT)).then_inc(free["V"], 1)
                wait_taken(dve, "V", ("RP",))
                dve.wait_ge(ones_set, 1)
                for e in range(EXPERTS):
                    ins = v.tensor_tensor_scan(inc[:, :, e], ones[:, 0:TT], tot[:, :, e], 0.0, ALU.mult, ALU.add)
                link(ins)
                cmp = tmp.rearrange("p t e -> p (t e)").rearrange("p (e k) -> p e k", e=EXPERTS)
                link(v.tensor_tensor(cmp, inc[:, TT - 1, :].unsqueeze(2).to_broadcast([P, EXPERTS, TT]),
                                     steps128.unsqueeze(1).to_broadcast([P, EXPERTS, TT]), ALU.is_gt))
                link(v.tensor_reduce(nt, cmp, AX.X, ALU.add))
                link(v.tensor_tensor_scan(end, ones[:, 0:EXPERTS], nt, 0.0, ALU.mult, ALU.add))
                link(v.tensor_tensor(off, end, nt, ALU.subtract))
                link(v.tensor_tensor(inc, inc, tot, ALU.subtract))
                v.tensor_tensor(slot, inc, bank["H"][:, 0:TT * EXPERTS].rearrange("p (t e) -> p t e", t=TT), ALU.add).then_inc(free["H"], 1)
                wait_taken(dve, "H", ("RP",))
                link(v.tensor_scalar(off, off, float(P), None, ALU.mult))
                link(v.tensor_tensor(slot, slot, off.unsqueeze(1).to_broadcast([P, TT, EXPERTS]), ALU.add))
                for oh, f, sl in ((oh1, f1, sl1), (oh2, f2, sl2)):
                    link(v.tensor_tensor(tmp, oh, slot, ALU.mult))
                    link(v.tensor_reduce(f, tmp, AX.X, ALU.add))
                    link(v.tensor_copy(sl[:, :], f))
                k = JT * EXPERTS
                big = v1[0:1, 20 * TT * EXPERTS:20 * TT * EXPERTS + k].rearrange("p (j e) -> p j e", e=EXPERTS)
                fl = v1[0:1, 24 * TT * EXPERTS:24 * TT * EXPERTS + JT]
                link(v.tensor_tensor(big, tiles[0:1, :].unsqueeze(2).to_broadcast([1, JT, EXPERTS]),
                                     end[0:1, :].unsqueeze(1).to_broadcast([1, JT, EXPERTS]), ALU.is_ge))
                link(v.tensor_reduce(fl, big, AX.X, ALU.add))
                link(v.tensor_scalar(fl, fl, float(EXPERTS - 1), float(WE), ALU.min, ALU.mult))
                link(v.tensor_copy(te[:, :], fl))
                assert done[0] == STAT_END, done

            def do(piece):
                kind = piece[0]
                if kind == "CV" and piece[2] in DVE_CONV:
                    e, c = piece[1], piece[2]
                    b = "G" if e < 2 else "V"
                    wait_taken(dve, b, ("B2", e // 2, c))
                    if c >= 1:
                        wait_full(dve, "V", ("B5", 0, c - 1))
                    first = 3 * (KE * len([k for k in DVE_CONV if k < c]) + e)
                    v.tensor_scalar(xc[:, e, :], xin[:, e, 0:CH], cw[:, e, 0:1], cb[:, e:e + 1],
                                    ALU.mult, ALU.add).then_inc(cvd, 1)
                    for w in range(1, TAPS):
                        dve.wait_ge(cvd, first + w)
                        v.scalar_tensor_tensor(out=xc[:, e, :], in0=xin[:, e, w:w + CH], scalar=cw[:, e, w:w + 1],
                                               in1=xc[:, e, :], op0=ALU.mult, op1=ALU.add).then_inc(cvd if w < TAPS - 1 else conv, 1)
                elif kind == "X2":
                    q, c = piece[1], piece[2]
                    dve.wait_ge(tqb, 2 * c + q + 1)
                    if q == 0 and c >= 2:
                        dve.wait_ge(uu, c - 1)
                    v.scalar_tensor_tensor(out=x2[:, c % 2, 2 * q:2 * q + 2, :], in0=tqB[:, :, :], scalar=1.0,
                                           in1=xc[:, 2 * q:2 * q + 2, :], op0=ALU.add, op1=ALU.mult).then_inc(x2r, 1)
                elif kind == "O1":
                    c = piece[2]
                    if c >= 1:
                        wait_full(dve, "V", ("O3", 1, c - 1))
                    dve.wait_ge(dlt, min(c + 2, CHUNKS))
                    for q, b in enumerate("HV"):
                        wait_full(dve, b, piece)
                        for i in range(2):
                            e = 2 * q + i
                            ins = v.scalar_tensor_tensor(out=y1[:, e, :], in0=x2[:, c % 2, e, :], scalar=WD[:, e:e + 1],
                                                         in1=bank[b][:, i * CH:(i + 1) * CH], op0=ALU.mult, op1=ALU.add)
                        ins.then_inc(free[b], 1)
                elif kind == "O2":
                    q, c = piece[1], piece[2]
                    dve.wait_ge(tqo, 2 * c + q + 1)
                    v.scalar_tensor_tensor(out=tqO[:, :, :], in0=tqO[:, :, :], scalar=1.0,
                                           in1=bank["G"][:, :].rearrange("p (k t) -> p k t", k=2),
                                           op0=ALU.add, op1=ALU.mult).then_inc(free["G"], 1)
                elif kind == "ST":
                    statistics(1)
                elif kind == "RA":
                    dve.wait_ge(wprep, 6)
                    router_choice()
                elif kind == "RB":
                    router_slots()
                elif kind == "FA" and piece[1] < JT:
                    j = piece[1]
                    dve.wait_ge(s_th, j + 1)
                    at_least(dve, s_g, j)
                    v.scalar_tensor_tensor(out=g1[:, :], in0=th[:, :], scalar=1.0, in1=bank["H"][:, :],
                                           op0=ALU.add, op1=ALU.mult).then_inc(free["H"], 1)
                elif kind == "S":
                    t = piece[1]
                    i = t % 2
                    dve.wait_ge(ld_s[i], 32 * (t // 2 + 1))
                    v.scalar_tensor_tensor(out=sbuf_m[i], in0=sbuf_x[i], scalar=r1[:, t:t + 1], in1=sbuf_m[i],
                                           op0=ALU.mult, op1=ALU.add).then_inc(sums, 1)
                    dve.wait_ge(gat[i], 32 * (t // 2 + 1))
                    for k, wt in enumerate((wt1, wt2)):
                        dve.wait_ge(sums, 3 * t + k + 1)
                        v.scalar_tensor_tensor(out=sbuf_m[i], in0=gbuf[i][:, k * D:(k + 1) * D], scalar=wt[:, t:t + 1],
                                               in1=sbuf_m[i], op0=ALU.mult, op1=ALU.add).then_inc(sums, 1)

            dve.wait_ge(ld_first, 16 * FIRST_LOADS)
            for piece in prologue():
                do(piece)
            for c in range(CHUNKS):
                at = pieces(c)
                for n in range(N):
                    u = N * c + n
                    scans(u)
                    for piece in at[2 * n]:
                        do(piece)
                    if u >= 1:
                        sum_states(u - 1)
                    for piece in at[2 * n + 1]:
                        do(piece)
            sum_states(N * CHUNKS - 1)
            for piece in epilogue():
                do(piece)


def kernel(L0_attn_resid, L0_attn_norm_w, L0_attn_skip_w, L0_attn_in_w, L0_attn_conv_w, L0_attn_conv_b, L0_attn_wd1,
           L0_attn_wd2, L0_attn_wd2_b, L0_attn_wB, L0_attn_wC, L0_attn_A_log, L0_attn_W_D, L0_attn_out_w,
           L0_ffn_Wr, L0_ffn_W1, L0_ffn_V1, L0_ffn_W2):
    import numpy as np
    import concourse.bacc as bacc
    from concourse.bass_utils import run_bass_kernel_spmd

    a = np.asarray
    column = lambda w: a(w).reshape(-1, P).T
    e_index = np.tile(np.arange(EXPERTS, dtype=np.float32), TT)
    table = np.concatenate([e_index, P * np.arange(TT, dtype=np.float32), np.arange(JT, dtype=np.float32)])
    arrays = {
        "x": a(L0_attn_resid), "norm_w": column(L0_attn_norm_w),
        "skip_wT": a(L0_attn_skip_w).T, "in_wT": a(L0_attn_in_w).T, "conv_w": a(L0_attn_conv_w),
        "conv_b": column(L0_attn_conv_b), "wd1T": a(L0_attn_wd1).T, "wd2T": a(L0_attn_wd2).T, "wd2_b": column(L0_attn_wd2_b),
        "wBCT": np.stack([a(L0_attn_wB).T, a(L0_attn_wC).T]), "A_log": a(L0_attn_A_log), "W_D": column(L0_attn_W_D),
        "out_wT": a(L0_attn_out_w).T, "Wr": a(L0_ffn_Wr), "W1": a(L0_ffn_W1), "V1": a(L0_ffn_V1), "W2": a(L0_ffn_W2),
        "ident": np.eye(P, dtype=np.float32), "tri": np.triu(np.ones((P, P), np.float32), 1),
        "cst": np.tile(table, (P, 1)),
    }
    arrays = {"in_" + k: np.ascontiguousarray(w) for k, w in arrays.items()}
    nc = bacc.Bacc("TRN2", target_bir_lowering=False, num_devices=1, dynamic_dma_scratch_size=8192)
    args = [nc.dram_tensor(k, w.shape, mybir.dt.from_np(w.dtype), kind="ExternalInput").ap() for k, w in arrays.items()]
    out = nc.dram_tensor("out_0", (BATCH, SEQ, D), F32, kind="ExternalOutput").ap()
    mamba_moe(nc, *args, out)
    r = run_bass_kernel_spmd(nc, [arrays], core_ids=[0])
    return r.results[0]["out_0"]
```

```python
import concourse.bass as bass
from concourse import mybir
from contextlib import ExitStack

F32 = mybir.dt.float32
I32 = mybir.dt.int32
ALU = mybir.AluOpType
ACT = mybir.ActivationFunctionType
AX = mybir.AxisListType

P = 128
BATCH, SEQ, D = 4, 1024, 256
E, N, R, TAPS = 512, 16, 128, 4
EXPERTS, FF, TOPK = 8, 512, 2
EPS = 1e-5
TOKENS = BATCH * SEQ
KD, KE = D // P, E // P
CH = 256
SUB = CH // P
CHUNKS = TOKENS // CH
CPB = SEQ // CH
TT = TOKENS // P
JT = TOKENS * TOPK // P + EXPERTS
GROUPS = ((0, SUB), (SUB, TT))
STAT_VAR, STAT_RMS, STAT_LN = (1, 19), (9, 27), (18, 36)
STAT_LOGITS, STAT_MASK, STAT_END = 39, 58, 76
SLOTS = JT * P
WE = KD * FF
assert WE == (FF // P) * D

B_PIECES = [("B1",), ("B2", 0), ("CV", 0), ("B2", 1), ("CV", 1), ("X2", 0), ("CV", 2), ("CV", 3), ("X2", 1), ("B3",), ("B4",), ("SP",), ("DL",), ("U",), ("B5",)]
B_PLACES = {
    0: [3, 5, 7, 8, 9, 10, 12, 14, 17, 18, 22, 23, 24, 24, 28],
    1: [5, 7, 7, 10, 10, 11, 12, 14, 15, 18, 20, 20, 20, 22, 27],
    14: [5, 7, 7, 9, 9, 10, 12, 14, 15, 17, 18, 20, 22, 23, 27],
    "other": [5, 7, 8, 9, 9, 10, 12, 14, 15, 18, 21, 23, 24, 26, 29],
}
O_PIECES = [("O1",), ("O2", 0), ("O2", 1), ("O3", 0), ("O3", 1)]
O_PLACES = {
    1: [2, 2, 5, 10, 17],
    14: [2, 2, 4, 11, 16],
    15: [2, 2, 5, 9, 13],
    "other": [2, 2, 4, 11, 13],
}
F_PLACES = {
    0: [1, 3, 4, 6, 8, 9, 11, 13, 13, 15, 16, 17, 20, 21, 21, 23, 25, 27],
    1: [1, 4, 6, 6, 9, 12, 13, 14, 16, 17, 19, 20, 21, 23, 24, 25, 31],
    14: [1, 5, 8, 10, 10, 13, 13, 14, 16, 16, 19, 20, 21, 22, 23, 25, 26, 28],
    15: [1, 4, 8, 9, 15, 16, 18, 21, 23, 24, 25, 26, 27, 29],
    "other": [0, 1, 7, 8, 10, 11, 13, 14, 15, 16, 20, 21, 22, 22, 24, 27, 28, 31],
}
RA_PLACES = [29, 29, 29, 30, 30, 30]
LAST_GATE = (25, 27)
DVE_CONV = (0, 1, 2, 14, 15)
ACT_PRODUCTS = {1: 2, 14: 2}
DVE_DELTA = (2,)
DVE_GATE = (0,)
RING = 8
FIRST_FFN, LAST_FFN = 2, 14
TPC = JT // (LAST_FFN - FIRST_FFN)
assert TPC * 3 == len(F_PLACES["other"])


def pieces(c):
    at = [[] for _ in range(2 * N)]

    def put(table, kinds, chunk):
        for place, kind in zip(table.get(c, table["other"]), kinds):
            at[place].append((kind + (chunk,)) if len(kind) > 1 else (kind[0], 0, chunk))

    if c >= 1:
        put(O_PLACES, O_PIECES, c - 1)
    if c + 1 < CHUNKS:
        put(B_PLACES, B_PIECES, c + 1)
    places = F_PLACES.get(c, F_PLACES["other"])
    if c == 0:
        work = [("R", i) for i in range(TT // 2 + 2)]
    elif c == 1:
        work = [("D", i) for i in range(TT // 2)] + [("FB", -1)]
    elif c < LAST_FFN:
        first = TPC * (c - FIRST_FFN)
        work = [(kind, first + k) for k in range(TPC) for kind in ("FA", "FB", "FC")]
    elif c == LAST_FFN:
        work = [("FA", JT), ("FC", JT)] + [("S", t) for t in range(len(places) - 2)]
    else:
        work = [("S", t) for t in range(TT - SUB - len(places), TT - SUB)]
    assert len(work) == len(places)
    for place, piece in zip(places, work):
        at[place].append(piece)
    if c == CHUNKS - 1:
        for q, place in enumerate(LAST_GATE):
            at[place].append(("O2", q, c))
    if c == 0:
        for place, kind in zip(RA_PLACES, ("RA", "RC", "RD", "RP", "RB", "RE")):
            at[place].append((kind,))
    return at


def prologue():
    b2 = [("B2", q, 0) for q in range(KE // 2)]
    convs = [("CV", e, 0) for e in range(KE)]
    x2 = [("X2", q, 0) for q in range(KE // 2)]
    return [("B1", 0, 0)] + b2 + convs + x2 + [(k, 0, 0) for k in ("B3", "B4", "SP", "DL", "U")] + [("ST",), ("B5", 0, 0)]


def gpsimd_products(u):
    return 2 * (u + 1) - scalar_products(u)


def scalar_products(u):
    return sum(share * min(max(u + 1 - N * c, 0), N) for c, share in ACT_PRODUCTS.items())


def epilogue():
    last = CHUNKS - 1
    return [("LD",), ("O1", 0, last), ("O3", 0, last), ("O3", 1, last)] + [("S", t) for t in range(TT - SUB, TT)]


def ahead(t):
    return [0, 1] if t == 0 else [t + 1] if t < TT - SUB else []


def banks_of(piece):
    kind = piece[0]
    if kind == "B2":
        return ["G"] if piece[1] == 0 else ["V"]
    if kind == "O3":
        return ["H"] if piece[1] == 0 else ["V"]
    if kind == "FA":
        return (["H"] if piece[1] < JT else []) + (["G"] if piece[1] > 0 else [])
    if kind == "FB":
        return (["V"] if piece[1] >= 0 else []) + (["X"] if piece[1] + 1 < JT else [])
    if kind == "FC":
        return ["X"] if piece[1] > 0 else []
    if kind == "R":
        return ["H", "V"] if 1 <= piece[1] <= TT // 2 else []
    return {"B1": ["G"], "B3": ["G"], "B4": ["H", "V"], "B5": ["H", "V"], "O1": ["H", "V"], "O2": ["G"],
            "RP": ["H", "V"]}.get(kind, [])


def count_uses():
    order = list(prologue())
    begins = {}
    uses, count = {}, {"H": 0, "V": 0, "X": 0, "G": 0}

    def walk(piece):
        for b in banks_of(piece):
            uses[b, piece] = count[b]
            count[b] += 1

    for piece in order:
        walk(piece)
    for c in range(CHUNKS):
        begins[c] = dict(count)
        for place in pieces(c):
            for piece in place:
                walk(piece)
    for piece in epilogue():
        walk(piece)
    return uses, begins


def mamba_moe(nc, x, norm_w, skip_wT, in_wT, conv_w, conv_b, wd1T, wd2T, wd2_b, wBCT, A_log, W_D, out_wT,
              Wr, W1, V1, W2, ident, tri, cst, out):
    USES, BEGINS = count_uses()
    ctx = ExitStack()
    with ctx:
        def sb(name, shape, dt=F32):
            return ctx.enter_context(nc.sbuf_tensor(name, shape, dt))

        def sem(name):
            return ctx.enter_context(nc.semaphore(name))

        xbuf = nc.dram_tensor("xbuf", (SLOTS, D), F32, kind="Internal").ap()
        ybuf = nc.dram_tensor("ybuf", (SLOTS, D), F32, kind="Internal").ap()
        mbuf = nc.dram_tensor("mbuf", (TOKENS, D), F32, kind="Internal").ap()
        x_rows = x.rearrange("b l d -> (b l) d")
        out_rows = out.rearrange("b l d -> (b l) d")

        w1 = sb("w1", [P, EXPERTS * WE])
        v1 = sb("v1", [P, EXPERTS * WE])
        w2 = sb("w2", [P, EXPERTS * WE])
        inw = sb("inw", [P, KD, E])
        skw = sb("skw", [P, KD, E])
        wd1 = sb("wd1", [P, KE, R])
        wd2 = sb("wd2", [P, E])
        wbc = sb("wbc", [P, KE, 2 * N])
        outw = sb("outw", [P, KE, D])
        wrt = sb("wrt", [P, KD, EXPERTS])
        cw = sb("cw", [P, KE, TAPS])
        cb = sb("cb", [P, KE])
        db = sb("db", [P, KE])
        Am = sb("Am", [P, KE, N])
        WD = sb("WD", [P, KE])
        nw = sb("nw", [P, KD])
        idn = sb("idn", [P, P])
        edge = sb("edge", [P, KE, TAPS - 1])
        st6 = sb("st6", [P, 2, 6])
        mv = sb("mv", [P, TT, 2])
        sq = sb("sq", [P, TT])
        ta = sb("ta", [P, TT])
        rstd = sb("rstd", [P, TT])
        nmr = sb("nmr", [P, TT])
        s2 = sb("s2", [P, TT])
        nm2 = sb("nm2", [P, TT])
        r1 = sb("r1", [P, TT])
        wt1 = sb("wt1", [P, TT])
        wt2 = sb("wt2", [P, TT])
        sl1 = sb("sl1", [P, TT], I32)
        sl2 = sb("sl2", [P, TT], I32)
        te = sb("te", [1, JT], I32)
        xch = sb("xch", [P, 2, SUB, D])
        rnT = sb("rnT", [P, 2, KD, CH])
        xin = sb("xin", [P, KE, TAPS - 1 + CH])
        xc = sb("xc", [P, KE, CH])
        tap = sb("tap", [P, 2, CH])
        tqB = sb("tqB", [P, 2, CH])
        tqO = sb("tqO", [P, 2, CH])
        x2 = sb("x2", [P, 2, KE, CH])
        delta = sb("delta", [P, 2, KE, CH])
        uT = sb("uT", [P, 2, SUB, E])
        yac = sb("yac", [P, 2, SUB, E])
        y1 = sb("y1", [P, KE, CH])
        BC = sb("BC", [P, 2, SUB, 2 * N])
        dtT = sb("dtT", [P, CH])
        carry = sb("carry", [P, N, KE])
        aexp = sb("aexp", [P, 2, KE, CH])
        ub = sb("ub", [P, 2, SUB, E])
        hb = sb("hb", [P, 2, KE, CH])
        tok = sb("tok", [P, 4, D])
        xT = sb("xT", [P, 2, KD, P])
        th = sb("th", [P, FF])
        g1 = sb("g1", [P, FF])
        vs = sb("vs", [P, FF])
        gT = sb("gT", [P, FF])
        mst = sb("mst", [P, 2, D])
        xall = w1[:, :].rearrange("p (t d) -> p t d", t=TT)
        rt = v1[:, :].rearrange("p (k t e) -> p k t e", k=WE * EXPERTS // (TT * EXPERTS), t=TT)
        trim = w2[:, 0:P]
        ones = w2[:, P:2 * P]
        csts = w2[:, 2 * P:2 * P + cst.shape[1]]

        bps = [ctx.enter_context(nc.psum_tensor(f"bps{i}", [P, 512], F32)) for i in range(2)]
        hps = [ctx.enter_context(nc.psum_tensor(f"hps{i}", [P, 512], F32)) for i in range(2)]
        bank = {b: ctx.enter_context(nc.psum_tensor(f"bank{b}", [P, 512], F32)) for b in "HVXG"}

        ld_first = sem("ld_first")
        ld_small = sem("ld_small")
        ld_late = sem("ld_late")
        ld_x = [sem(f"ld_x{i}") for i in range(4)]
        bst = sem("bst")
        ones_set = sem("ones_set")
        ld_w = sem("ld_w")
        ld_xch = [sem("ld_xch0"), sem("ld_xch1")]
        zero_set = sem("zero_set")
        zeroed = sem("zeroed")
        wprep = sem("wprep")
        aprep = sem("aprep")
        stat = sem("stat")
        sact = sem("sact")
        full = {b: sem("full_" + b) for b in "HVXG"}
        free = {b: sem("free_" + b) for b in "HVXG"}
        z_done = sem("z_done")
        halo = sem("halo")
        conv = sem("conv")
        cvs = sem("cvs")
        cvd = sem("cvd")
        tqb = sem("tqb")
        x2r = sem("x2r")
        dtr = sem("dtr")
        spx = sem("spx")
        dlt = sem("dlt")
        uu = sem("uu")
        tqo = sem("tqo")
        gate = sem("gate")
        m_out = [sem("m_out0"), sem("m_out1")]
        s_ub = sem("s_ub")
        s_uba = sem("s_uba")
        s_bT = sem("s_bT")
        s_a = sem("s_a")
        s_scan = sem("s_scan")
        s_cc = sem("s_cc")
        s_hT = sem("s_hT")
        s_acc = sem("s_acc")
        xn_r = sem("xn_r")
        xTr = sem("xTr")
        lgt = sem("lgt")
        disp = [sem(f"disp{i}") for i in range(RING)]
        ld_xs = [sem("ld_xs0"), sem("ld_xs1")]
        s_th = sem("s_th")
        s_g = sem("s_g")
        y_out = [sem("y_out0"), sem("y_out1")]
        gat = [sem(f"gat{i}") for i in range(2)]
        ld_s = [sem("ld_s0"), sem("ld_s1")]
        sums = sem("sums")
        o_out = [sem("o_out0"), sem("o_out1")]
        block = ctx.enter_context(nc.Block())

        gbuf = [g1[:, :], vs[:, :]]
        sbuf_x = [tok[:, 0, :], tok[:, 1, :]]
        sbuf_m = [tok[:, 2, :], tok[:, 3, :]]

        def at_least(eng, s, value):
            if value > 0:
                eng.wait_ge(s, value)

        def wait_full(eng, b, piece):
            at_least(eng, full[b], USES[b, piece] + 1)

        def wait_free(eng, b, piece):
            at_least(eng, free[b], USES[b, piece])

        def wait_taken(eng, b, piece):
            at_least(eng, free[b], USES[b, piece] + 1)

        def gate_place(q, c):
            return tqB[:, :, :] if q == 1 and c == CHUNKS - 1 else tqO[:, :, :]

        def add_delta(eng, ops, c):
            eng.wait_ge(spx, 6 * c + 6)
            wait_taken(eng, "V", ("B4", 0, c))
            ops.tensor_tensor(delta[:, c % 2, :, :], delta[:, c % 2, :, :], y1[:, :, :], ALU.add).then_inc(dlt, 1)

        def scale_by_delta(eng, ops, c):
            eng.wait_ge(dlt, c + 1)
            eng.wait_ge(x2r, 2 * c + 2)
            ops.tensor_tensor(xc[:, :, :], delta[:, c % 2, :, :], x2[:, c % 2, :, :], ALU.mult).then_inc(uu, 1)

        def apply_gate(eng, ops, q, c):
            wait_taken(eng, "G", ("O2", q, c))
            wait_taken(eng, "HV"[q], ("O1", 0, c))
            ops.tensor_tensor(y1[:, 2 * q:2 * q + 2, :], y1[:, 2 * q:2 * q + 2, :], gate_place(q, c),
                              ALU.mult).then_inc(gate, 1)

        FIRST_LOADS, SMALL_LOADS, LATE_LOADS = 5, 7, 5
        ring = [tok[:, k, :] for k in range(4)] + [g1[:, 0:D], g1[:, D:2 * D], vs[:, 0:D], vs[:, D:2 * D]]
        assert len(ring) == RING

        @block.sync
        def _(sp):
            def load_quarter(t):
                sp.dma_start(xall[:, t:t + 8, :], x_rows[t * P:(t + 8) * P, :].rearrange("(t p) d -> p t d", p=P)).then_inc(ld_x[t // 8], 16)

            def load_chunk(c):
                if c >= 2:
                    wait_full(sp, "G", ("B1", 0, c - 2))
                sp.dma_start(xch[:, c % 2, :, :], x_rows[c * CH:(c + 1) * CH, :].rearrange("(s p) d -> p s d", p=P)).then_inc(ld_xch[c % 2], 16)

            def load_tile(j):
                if j >= 2:
                    wait_full(sp, "X", ("FB", j - 3))
                sp.dma_start(tok[:, j % 2, :], xbuf[j * P:(j + 1) * P, :]).then_inc(ld_xs[j % 2], 16)

            def load_sum(t):
                i = t % 2
                at_least(sp, o_out[i], 16 * (t // 2))
                sp.dma_start(sbuf_x[i], x_rows[t * P:(t + 1) * P, :]).then_inc(ld_s[i], 16)
                if t < TT - SUB:
                    sp.wait_ge(m_out[i], 16 * (t // 2 + 1))
                    sp.dma_start(sbuf_m[i], mbuf[t * P:(t + 1) * P, :]).then_inc(ld_s[i], 16)

            def do(piece):
                kind = piece[0]
                if kind == "B1" and piece[2] + 1 < CHUNKS:
                    load_chunk(piece[2] + 1)
                elif kind == "O3":
                    s, c = piece[1], piece[2]
                    wait_taken(sp, "HV"[s], piece)
                    t = SUB * c + s
                    if c < CHUNKS - 1:
                        sp.dma_start(mbuf[t * P:(t + 1) * P, :], mst[:, s, :]).then_inc(m_out[s], 16)
                elif kind == "R" and piece[1] < 8:
                    sp.wait_ge(zero_set, 2)
                    a0, a1 = piece[1] * JT // 8, (piece[1] + 1) * JT // 8
                    sp.dma_start(xbuf.rearrange("(p a) d -> p a d", p=P)[:, a0:a1, :],
                                 gT[:, 0:D].unsqueeze(1).to_broadcast([P, a1 - a0, D])).then_inc(zeroed, 16)
                elif kind == "D" and piece[1] == TT // 2 - 1:
                    sp.wait_ge(xn_r, 2 * TT)
                    sp.dma_start(w1[:, :].rearrange("p (e k f) -> p e k f", e=EXPERTS, k=KD), W1.rearrange("e (k p) f -> p e k f", p=P)).then_inc(ld_w, 16)
                elif kind == "RE":
                    sp.wait_ge(stat, STAT_END)
                    sp.dma_start(v1[:, :].rearrange("p (e k f) -> p e k f", e=EXPERTS, k=KD), V1.rearrange("e (k p) f -> p e k f", p=P)).then_inc(ld_w, 16)
                    sp.dma_start(w2[:, :].rearrange("p (e k f) -> p e k f", e=EXPERTS, k=FF // P), W2.rearrange("e (k p) f -> p e k f", p=P)).then_inc(ld_w, 16)
                elif kind == "FB" and piece[1] == -1:
                    for i in range(RING):
                        sp.wait_ge(disp[i], 16 * 2 * TT // RING)
                    load_tile(0)
                    load_tile(1)
                elif kind == "FA" and piece[1] + 2 < JT:
                    load_tile(piece[1] + 2)
                elif kind == "FC" and piece[1] > 0:
                    j = piece[1] - 1
                    wait_taken(sp, "X", piece)
                    sp.dma_start(ybuf[j * P:(j + 1) * P, :], tok[:, 2 + j % 2, :]).then_inc(y_out[j % 2], 16)
                elif kind == "LD":
                    load_sum(TT - 1)
                elif kind == "S":
                    t = piece[1]
                    if t == 0:
                        for k in range(2):
                            sp.wait_ge(y_out[k], 16 * JT // 2)
                    for tn in ahead(t):
                        load_sum(tn)
                    sp.wait_ge(sums, 3 * (t + 1))
                    sp.dma_start(out_rows[t * P:(t + 1) * P, :], sbuf_m[t % 2]).then_inc(o_out[t % 2], 16)

            load_chunk(0)
            for done, loads in (
                (ld_first, [(inw[:, :, :], in_wT.rearrange("(k p) e -> p k e", p=P)),
                            (cw[:, :, :], conv_w.rearrange("(k p) w -> p k w", p=P)), (cb[:, :], conv_b)]),
                (ld_small, [(wbc[:, :, 0:N], wBCT[0].rearrange("(k p) n -> p k n", p=P)),
                            (wbc[:, :, N:2 * N], wBCT[1].rearrange("(k p) n -> p k n", p=P)),
                            (Am[:, :, :], A_log.rearrange("(k p) n -> p k n", p=P)),
                            (wd1[:, :, :], wd1T.rearrange("(k p) r -> p k r", p=P)),
                            (wd2[:, :], wd2T), (db[:, :], wd2_b), (WD[:, :], W_D)]),
            ):
                for dst, src in loads:
                    sp.dma_start(dst, src).then_inc(done, 16)
            for t in range(0, TT, 8):
                load_quarter(t)
            for dst, src in [(wrt[:, :, :], Wr.rearrange("(k p) e -> p k e", p=P)),
                             (outw[:, :, :], out_wT.rearrange("(k p) d -> p k d", p=P)),
                             (skw[:, :, :], skip_wT.rearrange("(k p) e -> p k e", p=P)),
                             (trim, tri), (csts, cst)]:
                sp.dma_start(dst, src).then_inc(ld_late, 16)
            for piece in prologue():
                do(piece)
            for c in range(CHUNKS):
                for place in pieces(c):
                    for piece in place:
                        do(piece)
            for piece in epilogue():
                do(piece)
            for i in range(2):
                sp.wait_ge(o_out[i], 16 * TT // 2)
                sp.wait_ge(m_out[i], 16 * (CHUNKS - 1))
                sp.wait_ge(y_out[i], 16 * JT // 2)

        @block.scalar
        def _(act):
            act.dma_start(idn[:, :], ident).then_inc(ld_first, 16)
            act.dma_start(nw[:, :], norm_w).then_inc(ld_first, 16)

            def roots(g):
                t0, t1 = GROUPS[g]
                for step in (STAT_VAR, STAT_RMS):
                    act.wait_ge(stat, step[g])
                    nc.scalar.activation(sq[:, t0:t1], ta[:, t0:t1], ACT.Sqrt).then_inc(sact, 1)
                act.wait_ge(stat, STAT_LN[g])

            roots(0)
            act.wait_ge(ld_first, 16 * FIRST_LOADS)

            def exps(u):
                c, n = divmod(u, N)
                if n == 0:
                    act.wait_ge(dlt, c + 1)
                for e in range(KE):
                    at_least(act, s_scan, 4 * (u - 2) + e + 1)
                    nc.scalar.activation(aexp[:, u % 2, e, :], delta[:, c % 2, e, :], ACT.Exp,
                                         scale=Am[:, e, n:n + 1]).then_inc(s_a, 1)
                if ACT_PRODUCTS.get(c, 0):
                    wait_taken(act, "V", ("B5", 0, c))
                    act.wait_ge(s_bT, 2 * (u - 1))
                    for s in range(SUB - ACT_PRODUCTS[c], SUB):
                        nc.scalar.activation(ub[:, u % 2, s, :], uT[:, c % 2, s, :], ACT.Identity,
                                             scale=BC[:, c % 2, s, n:n + 1]).then_inc(s_uba, 1)

            def do(piece):
                kind = piece[0]
                if kind == "B1":
                    c = piece[2]
                    act.wait_ge(ld_xch[c % 2], 16 * (c // 2 + 1))
                    for s in range(SUB):
                        t = SUB * c + s
                        nc.scalar.activation(xch[:, c % 2, s, :], xch[:, c % 2, s, :], ACT.Identity,
                                             bias=nm2[:, t:t + 1], scale=s2[:, t:t + 1]).then_inc(z_done, 1)
                    wait_full(act, "G", piece)
                    if c >= 2:
                        wait_full(act, "G", ("O2", 1, c - 2))
                    for k in range(KD):
                        ins = nc.scalar.activation(rnT[:, c % 2, k, :], bank["G"][:, k * CH:(k + 1) * CH], ACT.Identity,
                                                   scale=nw[:, k:k + 1])
                    ins.then_inc(free["G"], 1)
                elif kind == "B2":
                    q, c = piece[1], piece[2]
                    b = "G" if q == 0 else "V"
                    at_least(act, conv, KE * c)
                    if q == 0:
                        if c % CPB == 0:
                            if c == 0:
                                act.wait_ge(zero_set, 2)
                            src = edge[:, :, :]
                        else:
                            src = xin[:, :, CH:CH + TAPS - 1]
                        nc.scalar.activation(xin[:, :, 0:TAPS - 1], src, ACT.Copy).then_inc(halo, 1)
                    act.wait_ge(halo, c + 1)
                    wait_full(act, b, piece)
                    nc.scalar.activation(xin[:, 2 * q:2 * q + 2, TAPS - 1:], bank[b][:, :].rearrange("p (k t) -> p k t", k=2),
                                         ACT.Copy).then_inc(free[b], 1)
                elif kind == "X2":
                    q, c = piece[1], piece[2]
                    act.wait_ge(conv, KE * c + 2 * q + 2)
                    at_least(act, x2r, 2 * c + q)
                    nc.scalar.activation(tqB[:, :, :], xc[:, 2 * q:2 * q + 2, :], ACT.Tanh, scale=0.5).then_inc(tqb, 1)
                elif kind == "B3":
                    c = piece[2]
                    wait_full(act, "G", piece)
                    at_least(act, s_ub, gpsimd_products(N * (c - 1) - 1))
                    at_least(act, s_uba, scalar_products(N * (c - 1) - 1))
                    at_least(act, s_acc, 2 * N * (c - 1))
                    if c >= 1:
                        wait_full(act, "V", ("B4", 0, c - 1))
                    nc.scalar.activation(dtT[:, :], bank["G"][:, 0:CH], ACT.Copy)
                    nc.scalar.activation(BC[:, c % 2, :, :], bank["G"][:, CH:CH + SUB * 2 * N].rearrange("p (s n) -> p s n", s=SUB),
                                         ACT.Copy).then_inc(free["G"], 1)
                elif kind == "B4":
                    c = piece[2]
                    if c >= 1:
                        at_least(act, dlt, c)
                    if c >= 2:
                        wait_full(act, "V", ("O3", 1, c - 2))
                        act.wait_ge(uu, c - 1)
                    for q, b in enumerate("HV"):
                        wait_full(act, b, piece)
                        for i in range(2):
                            e = 2 * q + i
                            nc.scalar.activation(y1[:, e, :], bank[b][:, i * CH:(i + 1) * CH], ACT.Abs,
                                                 bias=db[:, e:e + 1]).then_inc(spx, 1)
                            ins = nc.scalar.activation(delta[:, c % 2, e, :], bank[b][:, i * CH:(i + 1) * CH], ACT.Relu,
                                                       bias=db[:, e:e + 1])
                        ins.then_inc(free[b], 1)
                elif kind == "SP":
                    c = piece[2]
                    act.wait_ge(spx, 6 * c + 4)
                    nc.scalar.activation(y1[:, :, :], y1[:, :, :], ACT.Exp, scale=-1.0).then_inc(spx, 1)
                    act.wait_ge(spx, 6 * c + 5)
                    nc.scalar.activation(y1[:, :, :], y1[:, :, :], ACT.Ln, bias=1.0).then_inc(spx, 1)
                elif kind == "B5":
                    c = piece[2]
                    at_least(act, s_ub, gpsimd_products(N * (c - 1) - 1))
                    at_least(act, s_uba, scalar_products(N * (c - 1) - 1))
                    for s, b in enumerate("HV"):
                        wait_full(act, b, piece)
                        nc.scalar.activation(uT[:, c % 2, s, :], bank[b][:, :], ACT.Copy).then_inc(free[b], 1)
                elif kind == "O2":
                    q, c = piece[1], piece[2]
                    wait_full(act, "G", piece)
                    if c < CHUNKS - 1:
                        at_least(act, gate, 2 * c + q)
                    else:
                        act.wait_ge(gate, 2 * c)
                        act.wait_ge(x2r, 2 * CHUNKS)
                    nc.scalar.activation(gate_place(q, c), bank["G"][:, :].rearrange("p (k t) -> p k t", k=2), ACT.Tanh,
                                         scale=0.5).then_inc(tqo, 1)
                elif kind == "O3":
                    s, c = piece[1], piece[2]
                    b = "HV"[s]
                    t = SUB * c + s
                    wait_full(act, b, piece)
                    at_least(act, m_out[s], 16 * c)
                    nc.scalar.activation(mst[:, s, :], bank[b][:, 0:D], ACT.Identity, bias=nmr[:, t:t + 1]).then_inc(free[b], 1)
                elif kind == "R":
                    i = piece[1]
                    if i < TT // 2:
                        if i >= 2:
                            wait_full(act, "V", ("R", i - 1))
                        for t in (2 * i, 2 * i + 1):
                            nc.scalar.activation(tok[:, t % 4, :], xall[:, t, :], ACT.Identity, bias=nmr[:, t:t + 1],
                                                 scale=rstd[:, t:t + 1]).then_inc(xn_r, 1)
                    if 1 <= i <= TT // 2:
                        for k, t in enumerate((2 * i - 2, 2 * i - 1)):
                            wait_full(act, "HV"[k], piece)
                            at_least(act, lgt, t - 1)
                            nc.scalar.activation(xT[:, k, :, :], bank["HV"[k]][:, 0:D].rearrange("p (k t) -> p k t", k=KD),
                                                 ACT.Copy).then_inc(free["HV"[k]], 1)
                elif kind == "RA":
                    act.wait_ge(stat, STAT_LOGITS)
                    nc.scalar.activation(rt[:, 1], rt[:, 0], ACT.Exp).then_inc(sact, 1)
                elif kind == "D":
                    for t in (2 * piece[1], 2 * piece[1] + 1):
                        if t < RING:
                            wait_full(act, "V", ("R", TT // 2))
                        else:
                            act.wait_ge(disp[t % RING], 16 * 2 * (t // RING))
                        nc.scalar.activation(ring[t % RING], xall[:, t, :], ACT.Identity, bias=nmr[:, t:t + 1],
                                             scale=rstd[:, t:t + 1]).then_inc(xn_r, 1)
                elif kind == "FA":
                    j = piece[1]
                    if j < JT:
                        wait_full(act, "H", piece)
                        nc.scalar.activation(th[:, :], bank["H"][:, :], ACT.Tanh, scale=0.5).then_inc(s_th, 1)
                    if j > 0:
                        wait_full(act, "G", piece)
                        if j > 1:
                            wait_full(act, "X", ("FC", j - 1))
                        nc.scalar.activation(gT[:, :], bank["G"][:, :], ACT.Copy).then_inc(free["G"], 1)
                elif kind == "FB":
                    j = piece[1]
                    if j + 1 < JT:
                        wait_full(act, "X", piece)
                        if j < 0:
                            act.wait_ge(lgt, TT)
                        nc.scalar.activation(xT[:, (j + 1) % 2, :, :], bank["X"][:, 0:D].rearrange("p (k t) -> p k t", k=KD),
                                             ACT.Copy).then_inc(free["X"], 1)
                    if j >= 0:
                        wait_full(act, "V", piece)
                        nc.scalar.activation(vs[:, :], bank["V"][:, :], ACT.Copy).then_inc(free["V"], 1)
                elif kind == "FC" and piece[1] > 0:
                    j = piece[1] - 1
                    wait_full(act, "X", piece)
                    if j < 2:
                        act.wait_ge(disp[2 + j % 2], 16 * 2 * TT // RING)
                    else:
                        act.wait_ge(y_out[j % 2], 16 * (j // 2))
                    nc.scalar.activation(tok[:, 2 + j % 2, :], bank["X"][:, 0:D], ACT.Copy).then_inc(free["X"], 1)

            for piece in prologue():
                if piece == ("X2", 0, 0):
                    act.wait_ge(ld_small, 16 * SMALL_LOADS)
                    nc.scalar.activation(Am[:, :, :], Am[:, :, :], ACT.Exp).then_inc(aprep, 1)
                if piece == ("ST",):
                    roots(1)
                do(piece)
            act.wait_ge(wprep, 5)
            exps(0)
            for c in range(CHUNKS):
                at = pieces(c)
                for n in range(N):
                    if N * c + n + 1 < N * CHUNKS:
                        exps(N * c + n + 1)
                    for piece in at[2 * n] + at[2 * n + 1]:
                        do(piece)
            for piece in epilogue():
                do(piece)

        @block.gpsimd
        def _(pool):
            nc.gpsimd.memset(gT[:, :], 0.0).then_inc(zero_set, 1)
            nc.gpsimd.memset(edge[:, :, :], 0.0).then_inc(zero_set, 1)
            pool.wait_ge(ld_small, 16 * SMALL_LOADS)
            for w, k in ((wd1[:, :, :], 0.5), (wbc[:, :, 0:N], 0.25), (wbc[:, :, N:2 * N], 0.5), (WD[:, :], 0.5)):
                nc.gpsimd.tensor_scalar(w, w, k, 1.0, ALU.mult, ALU.mult).then_inc(wprep, 1)
            pool.wait_ge(aprep, 1)
            nc.gpsimd.tensor_scalar(Am[:, :, :], Am[:, :, :], -1.0, 1.0, ALU.mult, ALU.mult).then_inc(wprep, 1)

            def products(u):
                c, n = divmod(u, N)
                if n == 0:
                    wait_taken(pool, "V", ("B5", 0, c))
                at_least(pool, s_bT, 2 * (u - 1))
                for s in range(SUB - ACT_PRODUCTS.get(c, 0)):
                    nc.gpsimd.tensor_scalar(ub[:, u % 2, s, :], uT[:, c % 2, s, :], BC[:, c % 2, s, n:n + 1], 1.0,
                                            ALU.mult, ALU.mult).then_inc(s_ub, 1)

            def gather(t):
                at_least(pool, sums, 3 * (t - 1))
                for k, sl in enumerate((sl1, sl2)):
                    nc.gpsimd.indirect_dma_start(
                        out=gbuf[t % 2][:, k * D:(k + 1) * D], out_offset=None, in_=ybuf,
                        in_offset=bass.IndirectOffsetOnAxis(ap=sl[:, t:t + 1], axis=0)).then_inc(gat[t % 2], 16)

            def do(piece):
                kind = piece[0]
                if kind == "R" and piece[1] == 2:
                    pool.wait_ge(ld_late, 16 * LATE_LOADS)
                    nc.gpsimd.tensor_scalar(outw[:, :, :], outw[:, :, :], 0.5, 1.0, ALU.mult, ALU.mult).then_inc(wprep, 1)
                elif kind == "CV" and piece[2] not in DVE_CONV:
                    e, c = piece[1], piece[2]
                    b = "G" if e < 2 else "V"
                    wait_taken(pool, b, ("B2", e // 2, c))
                    if c >= 1:
                        wait_full(pool, "V", ("B5", 0, c - 1))
                    first = 6 * (KE * (c - len([k for k in DVE_CONV if k < c])) + e)

                    def product(dst, w, add):
                        return nc.gpsimd.tensor_scalar(dst, xin[:, e, w:w + CH], cw[:, e, w:w + 1], add,
                                                       ALU.mult, ALU.mult if w else ALU.add)

                    product(xc[:, e, :], 0, cb[:, e:e + 1]).then_inc(cvs, 1)
                    product(tap[:, 0, :], 1, 1.0).then_inc(cvs, 1)
                    product(tap[:, 1, :], 2, 1.0).then_inc(cvs, 1)
                    pool.wait_ge(cvs, first + 3)
                    nc.gpsimd.tensor_tensor(xc[:, e, :], xc[:, e, :], tap[:, 0, :], ALU.add).then_inc(cvs, 1)
                    pool.wait_ge(cvs, first + 4)
                    product(tap[:, 0, :], 3, 1.0).then_inc(cvs, 1)
                    nc.gpsimd.tensor_tensor(xc[:, e, :], xc[:, e, :], tap[:, 1, :], ALU.add).then_inc(cvs, 1)
                    pool.wait_ge(cvs, first + 6)
                    nc.gpsimd.tensor_tensor(xc[:, e, :], xc[:, e, :], tap[:, 0, :], ALU.add).then_inc(conv, 1)
                    pool.wait_ge(conv, KE * c + e + 1)
                elif kind == "DL" and piece[2] not in DVE_DELTA:
                    add_delta(pool, nc.gpsimd, piece[2])
                elif kind == "U" and piece[2] not in DVE_DELTA:
                    scale_by_delta(pool, nc.gpsimd, piece[2])
                elif kind == "O2" and piece[2] < CHUNKS - 1 and piece[2] not in DVE_GATE:
                    apply_gate(pool, nc.gpsimd, piece[1], piece[2])
                elif kind == "O1" and piece[2] == CHUNKS - 1 and piece[2] not in DVE_GATE:
                    for q in range(2):
                        apply_gate(pool, nc.gpsimd, q, piece[2])
                elif kind == "D":
                    if piece[1] == 0:
                        pool.wait_ge(zeroed, 16 * 8)
                        pool.wait_ge(stat, STAT_END)
                    for t in (2 * piece[1], 2 * piece[1] + 1):
                        pool.wait_ge(xn_r, TT + t + 1)
                        for sl in (sl1, sl2):
                            nc.gpsimd.indirect_dma_start(
                                out=xbuf, out_offset=bass.IndirectOffsetOnAxis(ap=sl[:, t:t + 1], axis=0),
                                in_=ring[t % RING], in_offset=None).then_inc(disp[t % RING], 16)
                elif kind == "FB" and piece[1] >= 0:
                    j = piece[1]
                    wait_taken(pool, "V", piece)
                    wait_taken(pool, "H", ("FA", j))
                    nc.gpsimd.tensor_tensor(vs[:, :], g1[:, :], vs[:, :], ALU.mult).then_inc(s_g, 1)
                elif kind == "S":
                    t = piece[1]
                    if t == 0:
                        for k in range(2):
                            pool.wait_ge(y_out[k], 16 * JT // 2)
                    for tn in ahead(t):
                        gather(tn)
                elif kind == "LD":
                    gather(TT - 1)

            for piece in prologue():
                do(piece)
            products(0)
            for c in range(CHUNKS):
                at = pieces(c)
                for n in range(N):
                    u = N * c + n
                    if u + 1 < N * CHUNKS:
                        products(u + 1)
                    for piece in at[2 * n]:
                        do(piece)
                    pool.wait_ge(s_scan, 4 * u + 4)
                    nc.gpsimd.tensor_copy(carry[:, n, :], hb[:, u % 2, :, CH - 1]).then_inc(s_cc, 1)
                    for piece in at[2 * n + 1]:
                        do(piece)
            for piece in epilogue():
                do(piece)

        @block.tensor
        def _(pe):
            pe.wait_ge(ld_first, 16 * FIRST_LOADS)

            def turn_products(u):
                pe.wait_ge(s_ub, gpsimd_products(u))
                at_least(pe, s_uba, scalar_products(u))
                for q in range(2):
                    at_least(pe, s_scan, 4 * (u - 1) + 2 * q + 2)
                    for s in range(SUB):
                        for i in range(2):
                            e = 2 * q + i
                            mm = pe.transpose(bps[q][:, i * CH + s * P:i * CH + (s + 1) * P],
                                              ub[:, u % 2, s, e * P:(e + 1) * P], idn[:, :])
                    mm.then_inc(s_bT, 1)

            def turn_states(u):
                pe.wait_ge(s_scan, 4 * u + 4)
                for s in range(SUB):
                    at_least(pe, s_acc, 2 * (u - 1) + s + 1)
                    for e in range(KE):
                        mm = pe.transpose(hps[s][:, e * P:(e + 1) * P], hb[:, u % 2, e, s * P:(s + 1) * P], idn[:, :])
                    mm.then_inc(s_hT, 1)

            def do(piece):
                kind = piece[0]
                if kind == "B1":
                    c = piece[2]
                    wait_free(pe, "G", piece)
                    for s in range(SUB):
                        pe.wait_ge(z_done, SUB * c + s + 1)
                        for k in range(KD):
                            mm = pe.transpose(bank["G"][:, k * CH + s * P:k * CH + (s + 1) * P],
                                              xch[:, c % 2, s, k * P:(k + 1) * P], idn[:, :])
                    mm.then_inc(full["G"], 1)
                elif kind == "B2" or kind == "O2":
                    q, c = piece[1], piece[2]
                    b = "G" if q == 0 or kind == "O2" else "V"
                    w = inw if kind == "B2" else skw
                    wait_free(pe, b, piece)
                    wait_taken(pe, "G", ("B1", 0, c))
                    for i in range(2):
                        e = 2 * q + i
                        for k in range(KD):
                            mm = pe.matmul(bank[b][:, i * CH:(i + 1) * CH], w[:, k, e * P:(e + 1) * P],
                                           rnT[:, c % 2, k, :], start=(k == 0), stop=(k == KD - 1))
                    mm.then_inc(full[b], 1)
                elif kind == "B3":
                    c = piece[2]
                    wait_free(pe, "G", piece)
                    pe.wait_ge(x2r, 2 * c + 2)
                    if c == 0:
                        pe.wait_ge(wprep, 5)
                    for k in range(KE):
                        pe.matmul(bank["G"][:, 0:CH], wd1[:, k, :], x2[:, c % 2, k, :], start=(k == 0), stop=(k == KE - 1))
                    for s in range(SUB):
                        for k in range(KE):
                            mm = pe.matmul(bank["G"][:, CH + s * 2 * N:CH + (s + 1) * 2 * N], x2[:, c % 2, k, s * P:(s + 1) * P],
                                           wbc[:, k, :], start=(k == 0), stop=(k == KE - 1))
                    mm.then_inc(full["G"], 1)
                elif kind == "B4":
                    c = piece[2]
                    wait_taken(pe, "G", ("B3", 0, c))
                    for q, b in enumerate("HV"):
                        wait_free(pe, b, piece)
                        for i in range(2):
                            e = 2 * q + i
                            mm = pe.matmul(bank[b][:, i * CH:(i + 1) * CH], wd2[:, e * P:(e + 1) * P], dtT[:, :],
                                           start=True, stop=True)
                        mm.then_inc(full[b], 1)
                elif kind == "B5":
                    c = piece[2]
                    pe.wait_ge(uu, c + 1)
                    for s, b in enumerate("HV"):
                        wait_free(pe, b, piece)
                        for e in range(KE):
                            mm = pe.transpose(bank[b][:, e * P:(e + 1) * P], xc[:, e, s * P:(s + 1) * P], idn[:, :])
                        mm.then_inc(full[b], 1)
                elif kind == "O1":
                    c = piece[2]
                    pe.wait_ge(s_acc, 2 * N * (c + 1))
                    for q, b in enumerate("HV"):
                        wait_free(pe, b, piece)
                        for s in range(SUB):
                            for i in range(2):
                                e = 2 * q + i
                                mm = pe.transpose(bank[b][:, i * CH + s * P:i * CH + (s + 1) * P],
                                                  yac[:, c % 2, s, e * P:(e + 1) * P], idn[:, :])
                        mm.then_inc(full[b], 1)
                elif kind == "O3":
                    s, c = piece[1], piece[2]
                    b = "HV"[s]
                    wait_free(pe, b, piece)
                    pe.wait_ge(gate, 2 * c + 2)
                    if c == 0:
                        pe.wait_ge(wprep, 6)
                    for k in range(KE):
                        mm = pe.matmul(bank[b][:, 0:D], y1[:, k, s * P:(s + 1) * P], outw[:, k, :],
                                       start=(k == 0), stop=(k == KE - 1))
                    mm.then_inc(full[b], 1)
                elif kind == "R":
                    i = piece[1]
                    if i == 2:
                        pe.wait_ge(ld_late, 16 * LATE_LOADS)
                    if i >= 2:
                        for k, t in enumerate((2 * i - 4, 2 * i - 3)):
                            wait_taken(pe, "HV"[k], ("R", i - 1))
                            for kd in range(KD):
                                mm = pe.matmul(bank["X"][:, t * EXPERTS:(t + 1) * EXPERTS], xT[:, k, kd, :], wrt[:, kd, :],
                                               start=(kd == 0), stop=(kd == KD - 1))
                            mm.then_inc(lgt, 1)
                    if 1 <= i <= TT // 2:
                        for k, t in enumerate((2 * i - 2, 2 * i - 1)):
                            wait_free(pe, "HV"[k], piece)
                            pe.wait_ge(xn_r, t + 1)
                            for kd in range(KD):
                                mm = pe.transpose(bank["HV"[k]][:, kd * P:(kd + 1) * P], tok[:, t % 4, kd * P:(kd + 1) * P], idn[:, :])
                            mm.then_inc(full["HV"[k]], 1)
                elif kind == "RP":
                    pe.wait_ge(stat, STAT_MASK)
                    pe.wait_ge(ones_set, 1)
                    for b, w in (("H", trim), ("V", ones)):
                        wait_free(pe, b, piece)
                        pe.matmul(bank[b][:, 0:TT * EXPERTS], w, rt[:, 7].rearrange("p t e -> p (t e)"), start=True, stop=True).then_inc(full[b], 1)
                elif kind == "FA":
                    j = piece[1]
                    if j < JT:
                        if j == 0:
                            pe.wait_ge(ld_w, 48)
                        col = pe.value_load(te[0:1, j:j + 1], min_val=0, max_val=(EXPERTS - 1) * WE)
                        columns[j] = col
                        wait_taken(pe, "X", ("FB", j - 1))
                        wait_free(pe, "H", piece)
                        for k in range(KD):
                            mm = pe.matmul(bank["H"][:, :], xT[:, j % 2, k, :], w1[:, bass.ds(col + k * FF, FF)],
                                           start=(k == 0), stop=(k == KD - 1))
                        mm.then_inc(full["H"], 1)
                    if j > 0:
                        wait_free(pe, "G", piece)
                        pe.wait_ge(s_g, j)
                        for k in range(FF // P):
                            mm = pe.transpose(bank["G"][:, k * P:(k + 1) * P], vs[:, k * P:(k + 1) * P], idn[:, :])
                        mm.then_inc(full["G"], 1)
                elif kind == "FB":
                    j = piece[1]
                    if j + 1 < JT:
                        if j < 0:
                            pe.wait_ge(lgt, TT)
                        pe.wait_ge(ld_xs[(j + 1) % 2], 16 * ((j + 1) // 2 + 1))
                        wait_free(pe, "X", piece)
                        for k in range(KD):
                            mm = pe.transpose(bank["X"][:, k * P:(k + 1) * P], tok[:, (j + 1) % 2, k * P:(k + 1) * P], idn[:, :])
                        mm.then_inc(full["X"], 1)
                    if j >= 0:
                        wait_free(pe, "V", piece)
                        for k in range(KD):
                            mm = pe.matmul(bank["V"][:, :], xT[:, j % 2, k, :], v1[:, bass.ds(columns[j] + k * FF, FF)],
                                           start=(k == 0), stop=(k == KD - 1))
                        mm.then_inc(full["V"], 1)
                elif kind == "FC" and piece[1] > 0:
                    j = piece[1] - 1
                    wait_taken(pe, "G", ("FA", j + 1))
                    wait_free(pe, "X", piece)
                    for k in range(FF // P):
                        mm = pe.matmul(bank["X"][:, 0:D], gT[:, k * P:(k + 1) * P], w2[:, bass.ds(columns[j] + k * D, D)],
                                       start=(k == 0), stop=(k == FF // P - 1))
                    mm.then_inc(full["X"], 1)

            columns = {}
            for piece in prologue():
                do(piece)
            for c in range(CHUNKS):
                at = pieces(c)
                for n in range(N):
                    u = N * c + n
                    turn_products(u)
                    for piece in at[2 * n]:
                        do(piece)
                    if u >= 1:
                        turn_states(u - 1)
                    for piece in at[2 * n + 1]:
                        do(piece)
            turn_states(N * CHUNKS - 1)
            for piece in epilogue():
                do(piece)

        @block.vector
        def _(dve):
            done = [0]

            def link(ins):
                done[0] += 1
                ins.then_inc(stat, 1)
                dve.wait_ge(stat, done[0])

            v = nc.vector
            v.memset(ones, 1.0).then_inc(ones_set, 1)
            def statistics(g):
                t0, t1 = GROUPS[g]
                for t in range(t0, t1):
                    if g == 0:
                        dve.wait_ge(ld_xch[0], 16)
                    elif t == t0 or t % 8 == 0:
                        dve.wait_ge(ld_x[t // 8], 16)
                    at_least(dve, bst, 2 * t - 2)
                    v.bn_stats(st6[:, t % 2, :], xch[:, 0, t, :] if g == 0 else xall[:, t, :]).then_inc(bst, 1)
                    dve.wait_ge(bst, 2 * t + 1)
                    v.bn_aggr(mv[:, t, :], st6[:, t % 2, :]).then_inc(bst, 1)
                dve.wait_ge(bst, 2 * t1)
                mean, var = mv[:, t0:t1, 0], mv[:, t0:t1, 1]
                root, under, rs, s, r = (a[:, t0:t1] for a in (sq, ta, rstd, s2, r1))

                def inverse_root(dst):
                    link(v.reciprocal(dst, root))
                    link(v.tensor_tensor(root, dst, dst, ALU.mult))
                    link(v.tensor_tensor(root, root, under, ALU.mult))
                    link(v.tensor_scalar(root, root, -0.5, 1.5, ALU.mult, ALU.add))
                    link(v.tensor_tensor(dst, dst, root, ALU.mult))

                link(v.tensor_scalar(under, var, EPS, None, ALU.add))
                dve.wait_ge(sact, 2 * g + 1)
                inverse_root(rs)
                link(v.tensor_tensor(r, rs, rs, ALU.mult))
                link(v.tensor_tensor(r, r, var, ALU.mult))
                link(v.tensor_scalar(under, r, EPS, None, ALU.add))
                assert done[0] == STAT_RMS[g]
                dve.wait_ge(sact, 2 * g + 2)
                inverse_root(s)
                link(v.tensor_tensor(s, s, rs, ALU.mult))
                link(v.scalar_tensor_tensor(out=nmr[:, t0:t1], in0=mean, scalar=-1.0, in1=rs, op0=ALU.mult, op1=ALU.mult))
                link(v.scalar_tensor_tensor(out=nm2[:, t0:t1], in0=mean, scalar=-1.0, in1=s, op0=ALU.mult, op1=ALU.mult))
                link(v.tensor_scalar(r, rs, 1.0, None, ALU.add))
                assert done[0] == STAT_LN[g]

            statistics(0)

            def scans(u):
                c, n = divmod(u, N)
                at_least(dve, s_hT, 2 * (u - 1))
                at_least(dve, s_cc, u - 1)
                for e in range(KE):
                    dve.wait_ge(s_a, 4 * u + e + 1)
                    if e % 2 == 0:
                        dve.wait_ge(s_bT, 2 * u + e // 2 + 1)
                    first = 0.0 if c % CPB == 0 else carry[:, n, e:e + 1]
                    v.tensor_tensor_scan(hb[:, u % 2, e, :], aexp[:, u % 2, e, :], bps[e // 2][:, (e % 2) * CH:(e % 2 + 1) * CH],
                                         first, ALU.mult, ALU.add).then_inc(s_scan, 1)

            def sum_states(u):
                c, n = divmod(u, N)
                if n == 0 and c >= 2:
                    wait_full(dve, "V", ("O1", 0, c - 2))
                for s in range(SUB):
                    dve.wait_ge(s_hT, 2 * u + s + 1)
                    at_least(dve, s_acc, 2 * (u - 1) + s + 1)
                    scale = BC[:, c % 2, s, N + n:N + n + 1]
                    if n == 0:
                        ins = v.tensor_scalar(yac[:, c % 2, s, :], hps[s][:, :], scale, None, ALU.mult)
                    else:
                        ins = v.scalar_tensor_tensor(out=yac[:, c % 2, s, :], in0=hps[s][:, :], scalar=scale,
                                                     in1=yac[:, c % 2, s, :], op0=ALU.mult, op1=ALU.add)
                    ins.then_inc(s_acc, 1)

            lg, gt, eq, cand, oh1, gt2, oh2, msk = (rt[:, k] for k in range(8))
            m1, m2, id1, den = (rt[:, 8 + k].rearrange("p t e -> p (t e)")[:, 0:TT] for k in range(4))

            def wide(a):
                return a.unsqueeze(2).to_broadcast([P, TT, EXPERTS])

            def router_logits():
                dve.wait_ge(lgt, TT)
                link(v.tensor_copy(lg, bank["X"][:, 0:TT * EXPERTS].rearrange("p (t e) -> p t e", t=TT)))
                link(v.tensor_reduce(m1, lg, AX.X, ALU.max))
                link(v.tensor_tensor(lg, lg, wide(m1), ALU.subtract))
                assert done[0] == STAT_LOGITS, done

            def router_gates():
                dve.wait_ge(sact, 5)
                link(v.tensor_reduce(den, gt, AX.X, ALU.add))
                link(v.reciprocal(den, den))
                link(v.tensor_tensor(gt, gt, wide(den), ALU.mult))

            def router_pick(src, m, oh):
                eid = csts[:, 0:TT * EXPERTS].rearrange("p (t e) -> p t e", t=TT)
                link(v.tensor_reduce(m, src, AX.X, ALU.min))
                link(v.tensor_tensor(eq, src, wide(m), ALU.is_equal))
                link(v.scalar_tensor_tensor(out=cand.rearrange("p t e -> p (t e)"), in0=eq.rearrange("p t e -> p (t e)"), scalar=-100.0,
                                            in1=eid.rearrange("p t e -> p (t e)"), op0=ALU.mult, op1=ALU.add))
                link(v.tensor_reduce(id1, cand, AX.X, ALU.min))
                link(v.tensor_tensor(oh, cand, wide(id1), ALU.is_equal))

            def router_others():
                link(v.scalar_tensor_tensor(out=gt2.rearrange("p t e -> p (t e)"), in0=oh1.rearrange("p t e -> p (t e)"), scalar=2.0,
                                            in1=gt.rearrange("p t e -> p (t e)"), op0=ALU.mult, op1=ALU.add))

            def router_scores():
                link(v.tensor_tensor(den, m1, m2, ALU.add))
                link(v.reciprocal(den, den))
                link(v.scalar_tensor_tensor(out=wt1[:, :], in0=m1, scalar=0.5, in1=den, op0=ALU.mult, op1=ALU.mult))
                link(v.scalar_tensor_tensor(out=wt2[:, :], in0=m2, scalar=0.5, in1=den, op0=ALU.mult, op1=ALU.mult))
                link(v.tensor_tensor(msk, oh1, oh2, ALU.add))
                assert done[0] == STAT_MASK, done

            slot, tot, inc, tmp = rt[:, 0], rt[:, 1], rt[:, 2], rt[:, 3]
            nt, end, off = (rt[:, 12 + k].rearrange("p t e -> p (t e)")[:, 0:EXPERTS] for k in range(3))
            f1, f2 = (rt[:, 15 + k].rearrange("p t e -> p (t e)")[:, 0:TT] for k in range(2))

            def router_counts():
                steps128 = csts[:, TT * EXPERTS:TT * EXPERTS + TT]
                wait_full(dve, "H", ("RP",))
                wait_full(dve, "V", ("RP",))
                v.tensor_copy(tot, bank["V"][:, 0:TT * EXPERTS].rearrange("p (t e) -> p t e", t=TT)).then_inc(free["V"], 1)
                wait_taken(dve, "V", ("RP",))
                dve.wait_ge(ones_set, 1)
                for e in range(EXPERTS):
                    ins = v.tensor_tensor_scan(inc[:, :, e], ones[:, 0:TT], tot[:, :, e], 0.0, ALU.mult, ALU.add)
                link(ins)
                cmp = tmp.rearrange("p t e -> p (t e)").rearrange("p (e k) -> p e k", e=EXPERTS)
                link(v.tensor_tensor(cmp, inc[:, TT - 1, :].unsqueeze(2).to_broadcast([P, EXPERTS, TT]),
                                     steps128.unsqueeze(1).to_broadcast([P, EXPERTS, TT]), ALU.is_gt))
                link(v.tensor_reduce(nt, cmp, AX.X, ALU.add))
                link(v.tensor_tensor_scan(end, ones[:, 0:EXPERTS], nt, 0.0, ALU.mult, ALU.add))
                link(v.tensor_tensor(off, end, nt, ALU.subtract))
                link(v.tensor_tensor(inc, inc, tot, ALU.subtract))
                v.tensor_tensor(slot, inc, bank["H"][:, 0:TT * EXPERTS].rearrange("p (t e) -> p t e", t=TT), ALU.add).then_inc(free["H"], 1)
                wait_taken(dve, "H", ("RP",))

            def router_slots():
                tiles = csts[:, TT * EXPERTS + TT:TT * EXPERTS + TT + JT]
                link(v.tensor_scalar(off, off, float(P), None, ALU.mult))
                link(v.tensor_tensor(slot, slot, off.unsqueeze(1).to_broadcast([P, TT, EXPERTS]), ALU.add))
                for oh, f, sl in ((oh1, f1, sl1), (oh2, f2, sl2)):
                    link(v.tensor_tensor(tmp, oh, slot, ALU.mult))
                    link(v.tensor_reduce(f, tmp, AX.X, ALU.add))
                    link(v.tensor_copy(sl[:, :], f))
                k = JT * EXPERTS
                big = v1[0:1, 20 * TT * EXPERTS:20 * TT * EXPERTS + k].rearrange("p (j e) -> p j e", e=EXPERTS)
                fl = v1[0:1, 24 * TT * EXPERTS:24 * TT * EXPERTS + JT]
                link(v.tensor_tensor(big, tiles[0:1, :].unsqueeze(2).to_broadcast([1, JT, EXPERTS]),
                                     end[0:1, :].unsqueeze(1).to_broadcast([1, JT, EXPERTS]), ALU.is_ge))
                link(v.tensor_reduce(fl, big, AX.X, ALU.add))
                link(v.tensor_scalar(fl, fl, float(EXPERTS - 1), float(WE), ALU.min, ALU.mult))
                link(v.tensor_copy(te[:, :], fl))
                assert done[0] == STAT_END, done

            def do(piece):
                kind = piece[0]
                if kind == "CV" and piece[2] in DVE_CONV:
                    e, c = piece[1], piece[2]
                    b = "G" if e < 2 else "V"
                    wait_taken(dve, b, ("B2", e // 2, c))
                    if c >= 1:
                        wait_full(dve, "V", ("B5", 0, c - 1))
                    first = 3 * (KE * len([k for k in DVE_CONV if k < c]) + e)
                    v.tensor_scalar(xc[:, e, :], xin[:, e, 0:CH], cw[:, e, 0:1], cb[:, e:e + 1],
                                    ALU.mult, ALU.add).then_inc(cvd, 1)
                    for w in range(1, TAPS):
                        dve.wait_ge(cvd, first + w)
                        v.scalar_tensor_tensor(out=xc[:, e, :], in0=xin[:, e, w:w + CH], scalar=cw[:, e, w:w + 1],
                                               in1=xc[:, e, :], op0=ALU.mult, op1=ALU.add).then_inc(cvd if w < TAPS - 1 else conv, 1)
                elif kind == "X2":
                    q, c = piece[1], piece[2]
                    dve.wait_ge(tqb, 2 * c + q + 1)
                    if q == 0 and c >= 2:
                        dve.wait_ge(uu, c - 1)
                    v.scalar_tensor_tensor(out=x2[:, c % 2, 2 * q:2 * q + 2, :], in0=tqB[:, :, :], scalar=1.0,
                                           in1=xc[:, 2 * q:2 * q + 2, :], op0=ALU.add, op1=ALU.mult).then_inc(x2r, 1)
                elif kind == "O1":
                    c = piece[2]
                    if c == 0:
                        dve.wait_ge(wprep, 5)
                    if c >= 1:
                        wait_full(dve, "V", ("O3", 1, c - 1))
                    dve.wait_ge(dlt, min(c + 2, CHUNKS))
                    for q, b in enumerate("HV"):
                        wait_full(dve, b, piece)
                        for i in range(2):
                            e = 2 * q + i
                            ins = v.scalar_tensor_tensor(out=y1[:, e, :], in0=x2[:, c % 2, e, :], scalar=WD[:, e:e + 1],
                                                         in1=bank[b][:, i * CH:(i + 1) * CH], op0=ALU.mult, op1=ALU.add)
                        ins.then_inc(free[b], 1)
                        if c == CHUNKS - 1 and c in DVE_GATE:
                            apply_gate(dve, v, q, c)
                elif kind == "O2":
                    q, c = piece[1], piece[2]
                    dve.wait_ge(tqo, 2 * c + q + 1)
                    v.scalar_tensor_tensor(out=gate_place(q, c), in0=gate_place(q, c), scalar=1.0,
                                           in1=bank["G"][:, :].rearrange("p (k t) -> p k t", k=2),
                                           op0=ALU.add, op1=ALU.mult).then_inc(free["G"], 1)
                    if c < CHUNKS - 1 and c in DVE_GATE:
                        apply_gate(dve, v, q, c)
                elif kind == "DL" and piece[2] in DVE_DELTA:
                    add_delta(dve, v, piece[2])
                elif kind == "U" and piece[2] in DVE_DELTA:
                    scale_by_delta(dve, v, piece[2])
                elif kind == "ST":
                    statistics(1)
                elif kind == "RA":
                    dve.wait_ge(ld_late, 16 * LATE_LOADS)
                    router_logits()
                elif kind == "RC":
                    router_gates()
                    router_pick(gt, m1, oh1)
                    router_others()
                elif kind == "RD":
                    router_pick(gt2, m2, oh2)
                    router_scores()
                elif kind == "RB":
                    router_counts()
                elif kind == "RE":
                    router_slots()
                elif kind == "FA" and piece[1] < JT:
                    j = piece[1]
                    dve.wait_ge(s_th, j + 1)
                    at_least(dve, s_g, j)
                    v.scalar_tensor_tensor(out=g1[:, :], in0=th[:, :], scalar=1.0, in1=bank["H"][:, :],
                                           op0=ALU.add, op1=ALU.mult).then_inc(free["H"], 1)
                elif kind == "S":
                    t = piece[1]
                    i = t % 2
                    mamba = sbuf_m[i]
                    if t < TT - SUB:
                        dve.wait_ge(ld_s[i], 32 * (t // 2 + 1))
                    else:
                        dve.wait_ge(ld_s[i], 32 * (t // 2) + 16)
                        mamba = mst[:, i, :]
                        wait_taken(dve, "HV"[i], ("O3", i, CHUNKS - 1))
                        dve.wait_ge(o_out[i], 16 * (t // 2))
                    v.scalar_tensor_tensor(out=sbuf_m[i], in0=sbuf_x[i], scalar=r1[:, t:t + 1], in1=mamba,
                                           op0=ALU.mult, op1=ALU.add).then_inc(sums, 1)
                    dve.wait_ge(gat[i], 32 * (t // 2 + 1))
                    for k, wt in enumerate((wt1, wt2)):
                        dve.wait_ge(sums, 3 * t + k + 1)
                        v.scalar_tensor_tensor(out=sbuf_m[i], in0=gbuf[i][:, k * D:(k + 1) * D], scalar=wt[:, t:t + 1],
                                               in1=sbuf_m[i], op0=ALU.mult, op1=ALU.add).then_inc(sums, 1)

            dve.wait_ge(ld_first, 16 * FIRST_LOADS)
            for piece in prologue():
                do(piece)
            for c in range(CHUNKS):
                at = pieces(c)
                for n in range(N):
                    u = N * c + n
                    scans(u)
                    for piece in at[2 * n]:
                        do(piece)
                    if u >= 1:
                        sum_states(u - 1)
                    for piece in at[2 * n + 1]:
                        do(piece)
            sum_states(N * CHUNKS - 1)
            for piece in epilogue():
                do(piece)


def kernel(L0_attn_resid, L0_attn_norm_w, L0_attn_skip_w, L0_attn_in_w, L0_attn_conv_w, L0_attn_conv_b, L0_attn_wd1,
           L0_attn_wd2, L0_attn_wd2_b, L0_attn_wB, L0_attn_wC, L0_attn_A_log, L0_attn_W_D, L0_attn_out_w,
           L0_ffn_Wr, L0_ffn_W1, L0_ffn_V1, L0_ffn_W2):
    import numpy as np
    import concourse.bacc as bacc
    from concourse.bass_utils import run_bass_kernel_spmd

    a = np.asarray
    column = lambda w: a(w).reshape(-1, P).T
    e_index = np.tile(np.arange(EXPERTS, dtype=np.float32), TT)
    table = np.concatenate([e_index, P * np.arange(TT, dtype=np.float32), np.arange(JT, dtype=np.float32)])
    arrays = {
        "x": a(L0_attn_resid), "norm_w": column(L0_attn_norm_w),
        "skip_wT": a(L0_attn_skip_w).T, "in_wT": a(L0_attn_in_w).T, "conv_w": a(L0_attn_conv_w),
        "conv_b": column(L0_attn_conv_b), "wd1T": a(L0_attn_wd1).T, "wd2T": a(L0_attn_wd2).T, "wd2_b": column(L0_attn_wd2_b),
        "wBCT": np.stack([a(L0_attn_wB).T, a(L0_attn_wC).T]), "A_log": a(L0_attn_A_log), "W_D": column(L0_attn_W_D),
        "out_wT": a(L0_attn_out_w).T, "Wr": a(L0_ffn_Wr), "W1": a(L0_ffn_W1), "V1": a(L0_ffn_V1), "W2": a(L0_ffn_W2),
        "ident": np.eye(P, dtype=np.float32), "tri": np.triu(np.ones((P, P), np.float32), 1),
        "cst": np.tile(table, (P, 1)),
    }
    arrays = {"in_" + k: np.ascontiguousarray(w) for k, w in arrays.items()}
    nc = bacc.Bacc("TRN2", target_bir_lowering=False, num_devices=1, dynamic_dma_scratch_size=8192)
    args = [nc.dram_tensor(k, w.shape, mybir.dt.from_np(w.dtype), kind="ExternalInput").ap() for k, w in arrays.items()]
    out = nc.dram_tensor("out_0", (BATCH, SEQ, D), F32, kind="ExternalOutput").ap()
    mamba_moe(nc, *args, out)
    r = run_bass_kernel_spmd(nc, [arrays], core_ids=[0])
    return r.results[0]["out_0"]
```
